# Optimizing a Trainium2 kernel written in Bass

```python
import numpy as np
import jax
import jax.numpy as jnp

def _softmax(x, axis=-1):
    return jax.nn.softmax(x, axis=axis)

def _gelu(x):
    return jax.nn.gelu(x, approximate=True)

def _silu(x):
    return jax.nn.silu(x)

def _sigmoid(x):
    return jax.nn.sigmoid(x)

def _layernorm(x, axis=-1, eps=1e-05):
    m = jnp.mean(x, axis=axis, keepdims=True)
    v = jnp.var(x, axis=axis, keepdims=True)
    return (x - m) / jnp.sqrt(v + eps)

def _scatter_add(tgt, idx, src, axis=0):
    return tgt.at[idx].add(src)

def _segment_sum(src, seg, n):
    return jax.ops.segment_sum(src, seg, n)
kernel_name = 'mk_gnn_resnorm_d2_gnn_r8_44e15b'

def setup_inputs(seed: int=0):
    np.random.seed(seed)
    _w = jnp.asarray

    def _rec_inputs():
        import jax
        import jax.numpy as jnp
        _gk = jax.random.key(seed)
        x = -0.000202 + 1 * jax.random.normal(jax.random.fold_in(_gk, 1), (6250, 128), jnp.float32)
        src = jax.random.randint(jax.random.fold_in(_gk, 2), (100000,), 0, 6250, jnp.int32)
        dst = jnp.minimum((6250 * jax.random.uniform(jax.random.fold_in(_gk, 3), (100000,)) ** 2.0).astype(jnp.int32), 49999)
        _o = jnp.argsort(dst, stable=True)
        src = src[_o]
        dst = dst[_o]
        edge_type_8 = jax.random.randint(jax.random.fold_in(_gk, 12), (100000,), 0, 8, jnp.int32)
        return (x, src, dst, edge_type_8)
    x, src, dst, edge_type_8 = _rec_inputs()

    def _L0_gnn_setup():
        import jax, jax.numpy as jnp
        import numpy as np
        N, E = (6250, 100000)
        IN, HID, R, B, L = (128, 128, 8, 4, 3)
        EPS = 1e-05

        def _rgcn_conv(x, src, dst, etype, bases_l, comp_l, root_l, bias_l):
            weight = jnp.einsum('rb,bio->rio', comp_l, bases_l)
            h = jnp.einsum('ni,rio->nro', x, weight)
            msg = h[src, etype]
            seg = dst * R + etype
            cnt = jax.ops.segment_sum(jnp.ones((msg.shape[0],), dtype=x.dtype), seg, num_segments=N * R)
            norm = 1.0 / jnp.maximum(cnt[seg], 1.0)
            agg = jax.ops.segment_sum(msg * norm[:, None], dst, num_segments=N)
            return agg + x @ root_l + bias_l

        def _batch_norm(x, w, b):
            m = x.mean(axis=0)
            v = x.var(axis=0)
            return (x - m) * jax.lax.rsqrt(v + EPS) * w + b
        key = jax.random.key(seed)
        ks = jax.random.split(key, 8)
        x = jax.random.normal(ks[0], (N, IN), dtype=jnp.float32)
        edge_index = jax.random.randint(ks[1], (2, E), 0, N, dtype=jnp.int32)
        edge_type = jax.random.randint(ks[2], (E,), 0, R, dtype=jnp.int32)
        bases = jax.random.normal(ks[3], (L, B, IN, HID), dtype=jnp.float32) * 0.05
        comp = jax.random.normal(ks[4], (L, R, B), dtype=jnp.float32) * 0.3
        root = jax.random.normal(ks[5], (L, IN, HID), dtype=jnp.float32) * 0.05
        bias = jax.random.normal(ks[6], (L, HID), dtype=jnp.float32) * 0.01
        bn_weight = 1.0 + 0.1 * jax.random.normal(ks[7], (L - 1, HID), dtype=jnp.float32)
        bn_bias = jnp.zeros((L - 1, HID), dtype=jnp.float32)
        return dict(x=x, edge_index=edge_index, edge_type=edge_type, bases=bases, comp=comp, root=root, bias=bias, bn_weight=bn_weight, bn_bias=bn_bias)
    _L0_gnn_all = _L0_gnn_setup()
    _L0_gnn_in = {k: v for k, v in _L0_gnn_all.items() if k in ('bases', 'comp', 'root', 'bias', 'bn_weight', 'bn_bias')}
    del _L0_gnn_all

    def _L1_gnn_setup():
        import jax, jax.numpy as jnp
        import numpy as np
        NUM_LAYERS = 3
        key = jax.random.key(seed)
        k1, k2, k3, k4, k5, k6 = jax.random.split(key, 6)
        N, E, IN, H, OUT = (12500, 200000, 128, 64, 128)
        x = jax.random.normal(k1, (N, IN), dtype=jnp.float32)
        edge_index = jax.random.randint(k2, (2, E), 0, N, dtype=jnp.int64)
        W_in = jax.random.normal(k3, (IN, H), dtype=jnp.float32) / np.sqrt(IN)
        b_in = jax.random.normal(k4, (H,), dtype=jnp.float32) * 0.01
        W_out = jax.random.normal(k5, (H, OUT), dtype=jnp.float32) / np.sqrt(H)
        b_out = jax.random.normal(k6, (OUT,), dtype=jnp.float32) * 0.01
        return {'x': x, 'edge_index': edge_index, 'W_in': W_in, 'b_in': b_in, 'W_out': W_out, 'b_out': b_out}
    _L1_gnn_all = _L1_gnn_setup()
    _L1_gnn_in = {k: v for k, v in _L1_gnn_all.items() if k in ('W_in', 'b_in', 'W_out', 'b_out')}
    del _L1_gnn_all
    return {'x': x, 'src': src, 'dst': dst, 'edge_type_8': edge_type_8, 'L0_gnn_bases': _L0_gnn_in['bases'], 'L0_gnn_comp': _L0_gnn_in['comp'], 'L0_gnn_root': _L0_gnn_in['root'], 'L0_gnn_bias': _L0_gnn_in['bias'], 'L0_gnn_bn_weight': _L0_gnn_in['bn_weight'], 'L0_gnn_bn_bias': _L0_gnn_in['bn_bias'], 'L1_gnn_W_in': _L1_gnn_in['W_in'], 'L1_gnn_b_in': _L1_gnn_in['b_in'], 'L1_gnn_W_out': _L1_gnn_in['W_out'], 'L1_gnn_b_out': _L1_gnn_in['b_out']}

def reference(x, src, dst, edge_type_8, L0_gnn_bases, L0_gnn_comp, L0_gnn_root, L0_gnn_bias, L0_gnn_bn_weight, L0_gnn_bn_bias, L1_gnn_W_in, L1_gnn_b_in, L1_gnn_W_out, L1_gnn_b_out):
    import jax
    import jax.numpy as jnp

    def _L0_gnn_ref(x, edge_index, edge_type, bases, comp, root, bias, bn_weight, bn_bias):
        import jax, jax.numpy as jnp
        import numpy as np
        N, E = (6250, 100000)
        IN, HID, R, B, L = (128, 128, 8, 4, 3)
        EPS = 1e-05

        def _rgcn_conv(x, src, dst, etype, bases_l, comp_l, root_l, bias_l):
            weight = jnp.einsum('rb,bio->rio', comp_l, bases_l)
            h = jnp.einsum('ni,rio->nro', x, weight)
            msg = h[src, etype]
            seg = dst * R + etype
            cnt = jax.ops.segment_sum(jnp.ones((msg.shape[0],), dtype=x.dtype), seg, num_segments=N * R)
            norm = 1.0 / jnp.maximum(cnt[seg], 1.0)
            agg = jax.ops.segment_sum(msg * norm[:, None], dst, num_segments=N)
            return agg + x @ root_l + bias_l

        def _batch_norm(x, w, b):
            m = x.mean(axis=0)
            v = x.var(axis=0)
            return (x - m) * jax.lax.rsqrt(v + EPS) * w + b
        src, dst = (edge_index[0], edge_index[1])
        for l in range(L - 1):
            x = _rgcn_conv(x, src, dst, edge_type, bases[l], comp[l], root[l], bias[l])
            x = _batch_norm(x, bn_weight[l], bn_bias[l])
            x = jax.nn.relu(x)
        x = _rgcn_conv(x, src, dst, edge_type, bases[L - 1], comp[L - 1], root[L - 1], bias[L - 1])
        return x

    def _L1_gnn_ref(x, edge_index, W_in, b_in, W_out, b_out):
        import jax, jax.numpy as jnp
        import numpy as np
        NUM_LAYERS = 3
        N = x.shape[0]
        row, col = (edge_index[0], edge_index[1])
        h = x @ W_in + b_in
        deg = jax.ops.segment_sum(jnp.ones(row.shape[0], dtype=h.dtype), row, num_segments=N)
        deg_inv_sqrt = jnp.where(deg > 0, jax.lax.rsqrt(jnp.maximum(deg, 1.0)) * jnp.where(deg > 0, 1.0, 0.0), 0.0)
        edge_weight = deg_inv_sqrt[row] * deg_inv_sqrt[col]
        acc = h
        cur = h
        for _ in range(NUM_LAYERS):
            msgs = cur[col] * edge_weight[:, None]
            cur = jax.ops.segment_sum(msgs, row, num_segments=N)
            acc = acc + cur
        final = acc / (NUM_LAYERS + 1)
        return final @ W_out + b_out
    edge_index = jnp.stack([src, dst])
    x = _layernorm(x + _L0_gnn_ref(x, edge_index, edge_type_8, L0_gnn_bases, L0_gnn_comp, L0_gnn_root, L0_gnn_bias, L0_gnn_bn_weight, L0_gnn_bn_bias), axis=-1)
    x = _layernorm(x + _L1_gnn_ref(x, edge_index, L1_gnn_W_in, L1_gnn_b_in, L1_gnn_W_out, L1_gnn_b_out), axis=-1)
    return x

_drawn_inputs = setup_inputs


def setup_inputs(seed=0):
    import zlib

    import numpy as np

    out = dict(_drawn_inputs(seed))
    spreads = {'L0_gnn_bn_bias': (0.0, 0.1)}
    factors = {'L0_gnn_bias': 4.851, 'L1_gnn_b_in': 4.345, 'L1_gnn_b_out': 5.283}
    for name, (base, spread) in spreads.items():
        noise = np.random.default_rng([zlib.crc32(name.encode()), seed]).standard_normal(out[name].shape)
        drawn = base * np.exp(spread * noise) if base else spread * noise
        out[name] = jnp.asarray(drawn.astype(out[name].dtype))
    for name, factor in factors.items():
        out[name] = (out[name] * factor).astype(out[name].dtype)
    return out
```

```python
from contextlib import ExitStack

import numpy as np

import concourse.bass as bass
from concourse import mybir

ALU = mybir.AluOpType
ACT = mybir.ActivationFunctionType
F32 = mybir.dt.float32
F16 = mybir.dt.float16
BF16 = mybir.dt.bfloat16
I32 = mybir.dt.int32

N, E, D, H = 6250, 100000, 128, 64
R, BASES, LAYERS, HOPS = 8, 4, 3, 3
EPS = 1e-5

BW = 512
NB = -(-N // BW)
NP = NB * BW
NBLK = -(-N // 128)
NROW = NBLK * 128
LAST = N - (NBLK - 1) * 128

EP, EC = 125, 800
assert EP * EC == E

B = 16
Q = B // 2
NG = -(-(E // 256 + NB) // Q) * Q
NT = 2 * NG
NIT = NT // B
CH = 4
NCH = B // CH
SB = 8
PB = 4
GROUP = 2 * 128
NOKEY = 1023.0

NPAIR = R // 2
CROW = 2 * NBLK
CU = 8
SU = 16
SH = SU // 2
NSI = EC // SU
assert R == 2 * NPAIR and EC % CU == 0 and EC % SU == 0


def build(nc, x, src, dst, etype, bases, comp, root, bias, bn_w, bn_b, w_in, b_in, w_out, b_out, out):
    with ExitStack() as ctx:
        def sb(name, shape, dt=F32):
            return ctx.enter_context(nc.sbuf_tensor(name, shape, dt))

        def sem(name):
            return ctx.enter_context(nc.semaphore(name))

        def dram(name, shape, dt=F32):
            return nc.dram_tensor(name, shape, dt).ap()

        msg_table = dram("msg_table", (NROW * R, D))
        hop_table = dram("hop_table", (NROW, H))
        placed = {"dst": dram("placed_dst", (128 * NT, 2)), "src": dram("placed_src", (128 * NT, 2))}
        inv_count_dram = dram("inv_count", (3 * R * NROW,), BF16)
        inv_sqrt_dram = dram("inv_sqrt", (NROW,))

        xT = sb("xT", [128, NP])
        agg = sb("agg", [128, NP])
        cur = sb("cur", [128, NP])
        bufD = sb("bufD", [128, NP])
        bufE = sb("bufE", [128, NP])
        sel = sb("sel", [128, SB, BW])
        msg = sb("msg", [128, B, D])
        slots = sb("slots", [128, NT, 2])
        norm = sb("norm", [128, NT])
        payload = {k: sb(f"payload_{k}", [EP, EC, 2]) for k in ("dst", "src")}
        address = {k: sb(f"address_{k}", [EP, EC]) for k in ("dst", "src")}
        bucket = {k: sb(f"bucket_{k}", [1, NG], I32) for k in ("dst", "src")}
        weights = sb("weights", [128, R, D])
        bases_sb = sb("bases_sb", [128, BASES, D])
        comp_sb = sb("comp_sb", [128, LAYERS * R * BASES])
        root_sb = sb("root_sb", [128, LAYERS, D])
        bias_sb = sb("bias_sb", [128, LAYERS])
        bn_sb = sb("bn_sb", [128, 2, LAYERS - 1])
        w_in_sb = sb("w_in_sb", [128, H])
        w_out_sb = sb("w_out_sb", [H, D])
        b_in_sb = sb("b_in_sb", [H, 1])
        b_out_sb = sb("b_out_sb", [128, 1])
        iota = sb("iota", [128, BW])
        iota_types = sb("iota_types", [128, 3 * R])
        iota16 = sb("iota16", [128, R * NBLK], F16)
        iota_group = sb("iota_group", [1, NG])
        ident = sb("ident", [128, 128])
        ident16 = sb("ident16", [128, 128], BF16)
        ones = sb("ones", [128, 128])
        mean_w = sb("mean_w", [128, 128])
        earlier = sb("earlier", [128, 128])
        zeros16 = sb("zeros16", [128, 128], F16)
        eps = sb("eps", [128, 1])
        stage_idx = sb("stage_idx", [128, B], I32)
        stage_addr = sb("stage_addr", [EP, SU], I32)
        stage_pay = sb("stage_pay", [EP, SU, 2])
        hist = sb("hist", [EP, NB])
        small = sb("small", [128, 8, 16])
        small_i = sb("small_i", [128, 2, 16], I32)
        group_f = sb("group_f", [1, NG])
        stats = sb("stats", [128, NB, 6])
        moments = sb("moments", [128, 2])
        affine = sb("affine", [128, 4])

        def part(buf, at, cols, rows=EP, dt=F32):
            v = buf[0:rows, at:at + cols]
            return v if dt is F32 else v.bitcast(dt)

        src_i = part(bufD, 0, EC, dt=I32)
        dst_i = part(bufD, EC, EC, dt=I32)
        type_i = part(bufD, 2 * EC, EC, dt=I32)
        bucket_i = part(bufD, 3 * EC, EC, dt=I32)
        block_i = part(bufD, 4 * EC, EC, dt=I32)
        type_block = part(bufD, 5 * EC, EC)
        dst_low = part(bufD, 6 * EC, EC)
        src_low = part(bufD, 7 * EC, EC)
        inv_f = part(bufD, 0, 512, rows=CROW)
        rest_f = part(bufD, 512, 512, rows=CROW)
        inv_parts = part(bufD, 1024, 768, rows=CROW, dt=BF16).rearrange("p (a n) -> p a n", a=3)
        deg_f = part(bufD, 1800, 128, rows=NBLK)
        deg_r = part(bufD, 1928, 128, rows=NBLK)
        deg_out = part(bufD, 2056, 128, rows=NBLK)

        in_bucket = part(bufE, 0, EC)
        running = part(bufE, EC, EC)
        position = part(bufE, 2 * EC, EC)
        term = part(bufE, 3 * EC, EC)
        HOT = R * NBLK + 128 + NBLK + 128 + 1
        hot = part(bufE, 4 * EC, CU * HOT // 2, dt=F16).rearrange("p (u n) -> p u n", u=CU)
        inv_count = bufE[0:3 * R, 0:NP // 2].bitcast(BF16)
        AT = NP // 2
        type_rows = bufE[0:3 * R, AT:AT + NCH * BW // 2].bitcast(BF16).rearrange("p (c n) -> p c n", c=NCH)
        AT += NCH * BW // 2
        type_hot = bufE[:, AT:AT + B * 3 * R // 2].bitcast(BF16).rearrange("p (b n) -> p b n", b=B)
        AT += B * 3 * R // 2
        type_f = bufE[:, AT:AT + NT]
        type_t = cur[:, 0:NT].bitcast(I32)

        rows = cur[:, 0:NROW].rearrange("p (b d) -> p b d", d=D)
        staging = sel[:, :, :].rearrange("p s n -> p (s n)")
        table_stage = staging.rearrange("p (s n) -> p s n", s=4)
        hop_stage = staging.rearrange("p (s n) -> p s n", s=8)
        empty = staging[:, 0:2 * NT].rearrange("p (t w) -> p t w", w=2)

        psum = ctx.enter_context(nc.psum_tensor("psum", [128, 8, 512], F32))

        edges_in, params_in, rows_in, bases_in = sem("edges_in"), sem("params_in"), sem("rows_in"), sem("bases_in")
        constants = sem("constants")
        dve_step, act_step, pool_step = sem("dve_step"), sem("act_step"), sem("pool_step")
        empty_set, empty_out = sem("empty_set"), sem("empty_out")
        x_turned, x_kept = sem("x_turned"), sem("x_kept")
        hist_ready, base_ready = sem("hist_ready"), sem("base_ready")
        places_ready = sem("places_ready")
        hot_ready, counted = sem("hot_ready"), sem("counted")
        inv_ready, inv_out, deg_ready, root_ready = sem("inv_ready"), sem("inv_out"), sem("deg_ready"), sem("root_ready")
        deg_done, deg_out_s, inv_clear, inv_in = sem("deg_done"), sem("deg_out_s"), sem("inv_clear"), sem("inv_in")
        scale_clear, scale_in = sem("scale_clear"), sem("scale_in")
        staged_place = sem("staged_place")
        written = {k: [sem(f"written_{k}{h}") for h in range(2)] for k in ("dst", "src")}
        slots_in = sem("slots_in")
        slots_free = sem("slots_free")
        weights_ready = sem("weights_ready")
        table_mm, table_act, table_dve = sem("table_mm"), sem("table_act"), sem("table_dve")
        table_out = [sem(f"table_out{s}") for s in range(4)]
        tables_used = sem("tables_used")
        root_mm, root_kept = sem("root_mm"), sem("root_kept")
        staged = sem("staged")
        gathered = [sem(f"gathered{b}") for b in range(B)]
        sel_ready, summed, added = sem("sel_ready"), sem("summed"), sem("added")
        hot_types, types_turned, types_kept, weight_rows = sem("hot_types"), sem("types_turned"), sem("types_kept"), sem("weight_rows")
        var_ready, std_ready, affine_ready, act_layer = sem("var_ready"), sem("std_ready"), sem("affine_ready"), sem("act_layer")
        ln_in, ln_mean, ln_centred, ln_square = sem("ln_in"), sem("ln_mean"), sem("ln_centred"), sem("ln_square")
        ln_var, ln_std, ln_out = sem("ln_var"), sem("ln_std"), sem("ln_out")
        proj_mm, proj_kept, hop_scaled = sem("proj_mm"), sem("proj_kept"), sem("hop_scaled")
        hop_turned, hop_kept = sem("hop_turned"), sem("hop_kept")
        hop_out = [sem(f"hop_out{s}") for s in range(8)]
        agg_clear = sem("agg_clear")
        out_mm, out_biased = sem("out_mm"), sem("out_biased")
        out_turned, out_kept = sem("out_turned"), sem("out_kept")
        stored = sem("stored")
        passed = sem("passed")

        chunk = [slice(c * BW, (c + 1) * BW) for c in range(NB)]
        live = [slice(c * BW, min((c + 1) * BW, N)) for c in range(NB)]
        NXT = -(-NBLK // 4)
        HB = 7
        assert NBLK % HB == 0
        NHB = NBLK // HB
        CONVS = LAYERS + HOPS
        CONSTANTS = 14
        PARAMS = 6 + LAYERS + 2 * (LAYERS - 1)
        blocks_of = [range(4 * m, min(4 * m + 4, NBLK)) for m in range(NXT)]

        def turns(k, i):
            return NIT * k + i

        def apart(engine):
            engine.sem_inc(passed, 1)

        block = ctx.enter_context(nc.Block())

        @block.sync
        def _(sp):
            sp.dma_start(dst_i, dst.rearrange("(p c) -> p c", p=EP)).then_inc(edges_in, 16)
            sp.dma_start(type_i, etype.rearrange("(p c) -> p c", p=EP)).then_inc(edges_in, 16)
            sp.dma_start(src_i, src.rearrange("(p c) -> p c", p=EP)).then_inc(edges_in, 16)
            full = NBLK - 1
            sp.dma_start(rows[:, 0:full, :], x[0:full * 128, :].rearrange("(b p) d -> p b d", p=128)).then_inc(rows_in, 16)
            sp.dma_start(rows[0:LAST, full, :], x[full * 128:N, :]).then_inc(rows_in, 16)
            sp.wait_ge(empty_set, 2)
            for k in ("dst", "src"):
                sp.dma_start(placed[k].rearrange("(p t) w -> p (t w)", p=128), staging[:, 0:2 * NT]).then_inc(empty_out, 16)
            sp.dma_start(comp_sb[:, :], comp.rearrange("(a l) r b -> a (l r b)", a=1).to_broadcast([128, LAYERS * R * BASES])).then_inc(params_in, 16)
            sp.dma_start(root_sb[:, :, :], root.rearrange("l i o -> i l o")).then_inc(params_in, 16)
            for layer in range(LAYERS):
                sp.dma_start(bias_sb[:, layer:layer + 1], bias[layer].rearrange("(o a) -> o a", a=1)).then_inc(params_in, 16)
            for layer in range(LAYERS - 1):
                sp.dma_start(bn_sb[:, 0, layer:layer + 1], bn_w[layer].rearrange("(o a) -> o a", a=1)).then_inc(params_in, 16)
                sp.dma_start(bn_sb[:, 1, layer:layer + 1], bn_b[layer].rearrange("(o a) -> o a", a=1)).then_inc(params_in, 16)
            sp.dma_start(w_in_sb[:, :], w_in).then_inc(params_in, 16)
            sp.dma_start(w_out_sb[:, :], w_out).then_inc(params_in, 16)
            sp.dma_start(b_in_sb[:, :], b_in.rearrange("(p a) -> p a", a=1)).then_inc(params_in, 16)
            sp.dma_start(b_out_sb[:, :], b_out.rearrange("(p a) -> p a", a=1)).then_inc(params_in, 16)
            sp.dma_start(bases_sb[:, :, :], bases[0].rearrange("b i o -> i b o")).then_inc(bases_in, 16)

            sp.wait_ge(inv_ready, 1)
            for a in range(3):
                sp.dma_start(inv_count_dram.rearrange("(a j q n) -> a q j n", a=3, j=NPAIR, q=CROW)[a],
                             inv_parts[:, a, :].rearrange("p (j n) -> p j n", j=NPAIR)).then_inc(inv_out, 16)
            sp.wait_ge(deg_done, 1)
            sp.dma_start(inv_sqrt_dram.rearrange("(b n) -> b n", b=NBLK), deg_out).then_inc(deg_out_s, 16)
            sp.wait_ge(inv_out, 48)
            sp.wait_ge(inv_clear, 1)
            sp.dma_start(inv_count[:, 0:NROW], inv_count_dram.rearrange("(a n) -> a n", a=3 * R)).then_inc(inv_in, 16)

            def table(layer):
                for nb in range(NBLK):
                    n = NBLK * layer + nb
                    sp.wait_ge(table_act, n + 1)
                    sp.wait_ge(table_dve, n + 1)
                    sp.dma_start(msg_table[nb * 128 * R:(nb + 1) * 128 * R, :].rearrange("(p r) d -> p (r d)", r=R),
                                 table_stage[:, n % 4, :]).then_inc(table_out[n % 4], 16)

            def load_slots(k):
                for h in range(2):
                    sp.wait_ge(written[k][h], 16 * SH * NSI)
                sp.dma_start(slots[:, :, :].rearrange("p t w -> p (t w)"),
                             placed[k].rearrange("(p t) w -> p (t w)", p=128)).then_inc(slots_in, 16)

            table(0)
            load_slots("dst")
            for layer in range(1, LAYERS):
                sp.wait_ge(weights_ready, layer)
                sp.dma_start(bases_sb[:, :, :], bases[layer].rearrange("b i o -> i b o")).then_inc(bases_in, 16)
                table(layer)
            sp.wait_ge(scale_clear, 1)
            sp.wait_ge(deg_out_s, 16)
            sp.dma_start(bufE[0:H, 0:NROW], inv_sqrt_dram.rearrange("(a n) -> a n", a=1).to_broadcast([H, NROW])).then_inc(scale_in, 16)
            sp.wait_ge(added, PB + Q * turns(LAYERS, 0))
            load_slots("src")
            for hop in range(HOPS):
                for m in range(NHB):
                    n = NHB * hop + m
                    sp.wait_ge(hop_kept, n + 1)
                    sp.dma_start(hop_table[m * HB * 128:(m + 1) * HB * 128, :].rearrange("(b p) d -> p b d", p=128),
                                 hop_stage[:, m, 0:HB * H].rearrange("p (b d) -> p b d", d=H)).then_inc(hop_out[m], 16)
            for m in range(NXT):
                sp.wait_ge(out_kept, m + 1)
                bl = blocks_of[m]
                nfull = sum((b + 1) * 128 <= N for b in bl)
                if nfull:
                    sp.dma_start(out[bl[0] * 128:(bl[0] + nfull) * 128, :].rearrange("(b p) d -> p b d", p=128),
                                 cur[:, m * BW:m * BW + nfull * D].rearrange("p (b d) -> p b d", d=D)).then_inc(stored, 16)
                else:
                    sp.dma_start(out[bl[0] * 128:N, :], cur[0:LAST, m * BW:m * BW + D]).then_inc(stored, 16)
            sp.wait_ge(stored, 16 * NXT)

        @block.gpsimd
        def _(pool):
            g = nc.gpsimd
            g.memset(empty[:, :, 0], 0.0).then_inc(empty_set, 1)
            g.memset(empty[:, :, 1], NOKEY).then_inc(empty_set, 1)
            g.memset(ones[:, :], 1.0).then_inc(constants, 1)
            g.memset(ident[:, :], 0.0).then_inc(constants, 1)
            g.memset(ident16[:, :], 0.0).then_inc(constants, 1)
            g.memset(zeros16[:, :], 0.0).then_inc(constants, 1)
            g.memset(eps[:, :], EPS).then_inc(constants, 1)
            g.memset(mean_w[:, :], 1.0 / D).then_inc(constants, 1)
            g.iota(iota[:, :], [[1, BW]], base=0, channel_multiplier=0, allow_small_or_imprecise_dtypes=True).then_inc(constants, 1)
            g.iota(iota16[:, :], [[1, R * NBLK]], base=0, channel_multiplier=0, allow_small_or_imprecise_dtypes=True).then_inc(constants, 1)
            g.iota(iota_group[:, :], [[1, NG]], base=0, channel_multiplier=0, allow_small_or_imprecise_dtypes=True).then_inc(constants, 1)
            g.iota(iota_types[:, :], [[0, 3], [1, R]], base=0, channel_multiplier=0, allow_small_or_imprecise_dtypes=True).then_inc(constants, 1)
            pool.wait_ge(constants, 10)
            for m in (ident, ident16):
                g.affine_select(out=m[:, :], in_=m[:, :], compare_op=ALU.not_equal, fill=1.0, base=0,
                                pattern=[[-1, 128]], channel_multiplier=1).then_inc(constants, 1)
            g.affine_select(out=earlier[:, :], in_=ones[:, :], compare_op=ALU.is_gt, fill=0.0, base=0,
                            pattern=[[1, 128]], channel_multiplier=-1).then_inc(constants, 1)
            g.memset(norm[:, :], 0.0).then_inc(constants, 1)

            places = {"dst": 0, "src": 0}

            def place(k, first, last):
                def turn(i, peeled=False):
                    for h in range(2):
                        if not peeled:
                            pool.wait_ge(written[k][h], 16 * SH * i)
                        here = slice(h * SH, (h + 1) * SH)
                        base = 4 * (NSI if k == "src" else 0)
                        g.tensor_copy(stage_addr[:, here], address[k][:, bass.ds(SU * i + h * SH, SH)]).then_inc(staged_place, 1)
                        g.tensor_copy(stage_pay[:, here, :], payload[k][:, bass.ds(SU * i + h * SH, SH), :]).then_inc(staged_place, 1)
                        pool.wait_ge(staged_place, base + 4 * i + 2 * h + 2)
                        apart(pool)
                        for c in range(h * SH, (h + 1) * SH):
                            g.indirect_dma_start(out=placed[k], out_offset=bass.IndirectOffsetOnAxis(ap=stage_addr[:, c:c + 1], axis=0),
                                                 in_=stage_pay[:, c, :], in_offset=None).then_inc(written[k][h], 16)
                if first == 0:
                    turn(0, peeled=True)
                    first = 1
                with pool.Fori(first, last) as i:
                    turn(i)

            def gather(k):
                table, width = (msg_table, D) if k < LAYERS else (hop_table, H)
                with pool.Fori(0, NIT) as i:
                    for b in range(B):
                        if b % CH == 0:
                            pool.wait_ge(staged, NCH * turns(k, i) + b // CH + 1)
                        pool.wait_ge(summed, B * turns(k, i) + b + 1)
                        apart(pool)
                        g.indirect_dma_start(out=msg[:, b, 0:width], out_offset=None, in_=table,
                                             in_offset=bass.IndirectOffsetOnAxis(ap=stage_idx[:, b:b + 1], axis=0)).then_inc(gathered[b], 16)

            def squares(n):
                for c in range(NB):
                    at = NB * n + c
                    pool.wait_ge(ln_centred, at + 1)
                    if c >= 4:
                        pool.wait_ge(ln_var, at - 3)
                    g.tensor_tensor(sel[:, c % 4, :], agg[:, chunk[c]], agg[:, chunk[c]], ALU.mult).then_inc(ln_square, 1)

            pool.wait_ge(empty_out, 32)
            pool.wait_ge(places_ready, 1)
            place("dst", 0, NSI)
            cuts = [0, NSI // 3, 2 * NSI // 3, NSI]
            pool.wait_ge(places_ready, 2)
            for k in range(LAYERS):
                for s in range(4):
                    pool.wait_ge(table_out[s], 16 * len(range(s, NBLK * (k + 1), 4)))
                gather(k)
                if k == 0:
                    for h in range(2):
                        pool.wait_ge(written["dst"][h], 16 * SH * NSI)
                place("src", cuts[k], cuts[k + 1])
            squares(0)
            for hop in range(HOPS):
                for m in range(NHB):
                    pool.wait_ge(hop_out[m], 16 * (hop + 1))
                gather(LAYERS + hop)
            squares(1)

        @block.scalar
        def _(act):
            a = nc.scalar

            def stage(i, c):
                a.copy(stage_idx[:, c * CH:(c + 1) * CH], slots[:, bass.ds(B * i + c * CH, CH), 0]).then_inc(staged, 1)

            def conv(k):
                if k in (0, LAYERS):
                    act.wait_ge(slots_in, 16 if k == 0 else 32)
                if k == 0:
                    act.sem_inc(types_kept, 2)
                for c in range(NCH):
                    if k:
                        for b in range(c * CH, (c + 1) * CH):
                            act.wait_ge(gathered[b], 16 * turns(k, 0))
                    stage(0, c)

                def turn(i, ahead):
                    for c in range(NCH):
                        if k == 0:
                            act.wait_ge(types_turned, NCH + NCH * i + c + 1)
                            act.wait_ge(weight_rows, B * i + (c + 1) * CH)
                            a.copy(type_rows[:, c, :], psum[0:3 * R, 6 + c % 2, :]).then_inc(types_kept, 1)
                        if ahead:
                            for b in range(c * CH, (c + 1) * CH):
                                act.wait_ge(gathered[b], 16 * (turns(k, i) + 1))
                            stage(i + 1, c)
                with act.Fori(0, NIT - 1) as i:
                    turn(i, True)
                turn(NIT - 1, False)

            def table(layer):
                for nb in range(NBLK):
                    n = NBLK * layer + nb
                    act.wait_ge(table_mm, n + 1)
                    if n >= 4:
                        act.wait_ge(table_out[n % 4], 16 * (n // 4))
                    a.copy(table_stage[:, n % 4, 0:512], psum[:, 2 * (n % 4), :]).then_inc(table_act, 1)

            def root_part(layer):
                for c in range(NB):
                    act.wait_ge(root_mm, NB * layer + c + 1)
                    a.activation(agg[:, chunk[c]], psum[:, c % 8, :], ACT.Identity, bias=bias_sb[:, layer:layer + 1]).then_inc(root_kept, 1)

            act.wait_ge(params_in, 16 * PARAMS)
            act.wait_ge(constants, CONSTANTS)
            for m in range(NXT):
                act.wait_ge(x_turned, m + 1)
                w = len(blocks_of[m]) * 128 if m < NXT - 1 else LAST
                a.copy(xT[:, m * BW:m * BW + w], psum[:, m % 4, 0:w]).then_inc(x_kept, 1)
            act.wait_ge(deg_ready, 1)
            a.activation(deg_r, deg_r, ACT.Sqrt).then_inc(root_ready, 1)
            act.wait_ge(empty_out, 32)
            table(0)
            root_part(0)
            for layer in range(LAYERS):
                conv(layer)
                if layer == LAYERS - 1:
                    break
                act.wait_ge(var_ready, layer + 1)
                a.activation(affine[:, 0:1], moments[:, 1:2], ACT.Sqrt, bias=eps[:, 0:1]).then_inc(std_ready, 1)
                act.wait_ge(affine_ready, layer + 1)
                for c in range(NB):
                    a.activation(cur[:, live[c]], agg[:, live[c]], ACT.Relu, bias=affine[:, 3:4], scale=affine[:, 2:3]).then_inc(act_layer, 1)
                table(layer + 1)
                root_part(layer + 1)

            def deviations(n):
                for c in range(NB):
                    at = NB * n + c
                    act.wait_ge(ln_var, at + 1)
                    if c >= 4:
                        act.wait_ge(ln_out, at - 3)
                    a.activation(sel[:, 4 + c % 4, :], psum[:, 4 + c % 4, :], ACT.Sqrt, bias=eps[:, 0:1]).then_inc(ln_std, 1)

            deviations(0)
            for c in range(NB):
                act.wait_ge(proj_mm, c + 1)
                a.activation(cur[0:H, chunk[c]], psum[0:H, c % 4, :], ACT.Identity, bias=b_in_sb[:, 0:1]).then_inc(proj_kept, 1)
            for hop in range(HOPS):
                for m in range(NHB):
                    act.wait_ge(hop_turned, NHB * hop + m + 1)
                    if hop:
                        act.wait_ge(hop_out[m], 16 * hop)
                    a.copy(hop_stage[:, m, 0:HB * H], psum[:, m, 0:HB * H]).then_inc(hop_kept, 1)
                conv(LAYERS + hop)
            for c in range(NB):
                act.wait_ge(out_mm, c + 1)
                a.activation(cur[:, chunk[c]], psum[:, c % 8, :], ACT.Identity, bias=b_out_sb[:, 0:1], scale=1.0 / (HOPS + 1)).then_inc(out_biased, 1)
            deviations(1)
            for m in range(NXT):
                act.wait_ge(out_turned, m + 1)
                w = len(blocks_of[m]) * D
                a.copy(cur[:, m * BW:m * BW + w], psum[:, m % 4, 0:w]).then_inc(out_kept, 1)

        @block.tensor
        def _(pe):
            t = nc.tensor
            pe.sem_inc(summed, B)
            pe.sem_inc(added, PB)
            pe.sem_inc(types_turned, NCH)
            pe.sem_inc(weight_rows, B)
            pe.wait_ge(constants, CONSTANTS)
            pe.wait_ge(rows_in, 32)
            for m in range(NXT):
                if m >= 4:
                    pe.wait_ge(x_kept, m - 3)
                for j, nb in enumerate(blocks_of[m]):
                    p = 128 if nb < NBLK - 1 else LAST
                    last = t.transpose(psum[:, m % 4, j * 128:j * 128 + p], rows[0:p, nb, :], ident[0:p, 0:p])
                last.then_inc(x_turned, 1)

            def edges_before(n):
                pe.wait_ge(hist_ready, n + 1)
                t.matmul(psum[0:EP, 6, 0:NB], earlier[0:EP, 0:EP], hist[:, :], start=True, stop=True)
                t.matmul(psum[0:EP, 7, 0:NB], ones[0:EP, 0:EP], hist[:, :], start=True, stop=True).then_inc(base_ready, 1)

            edges_before(0)


            def count(u, first=False):
                h = hot[:, u, :]
                o = R * NBLK
                for j in range(NPAIR):
                    t.matmul(psum[0:CROW, 4, j * 128:(j + 1) * 128], h[:, j * CROW:(j + 1) * CROW], h[:, o:o + 128],
                             start=first and j == 0, stop=False, skip_group_check=True)
                t.matmul(psum[0:NBLK, 5, 0:128], h[:, o + 128:o + 128 + NBLK], h[:, o + 129 + NBLK:o + 257 + NBLK],
                         start=first, stop=False, skip_group_check=True).then_inc(counted, 1)

            def count_turn(i, first=False):
                for u in range(CU):
                    pe.wait_ge(hot_ready, CU * i + u + 1)
                    count(u, first and u == 0)
            count_turn(0, True)
            with pe.Fori(1, EC // CU) as i:
                count_turn(i)
            t.matmul(psum[0:CROW, 4, :], zeros16[0:EP, 0:CROW], hot[:, 0, 0:512], start=False, stop=True, skip_group_check=True)
            t.matmul(psum[0:NBLK, 5, 0:128], zeros16[0:EP, 0:NBLK], hot[:, 0, 0:128], start=False, stop=True,
                     skip_group_check=True).then_inc(counted, 1)
            edges_before(1)

            def table(layer, source):
                if layer == 0:
                    pe.wait_ge(x_kept, NXT)
                    pe.wait_ge(inv_ready, 1)
                    pe.wait_ge(deg_ready, 1)
                pe.wait_ge(weights_ready, layer + 1)
                for nb in range(NBLK):
                    n = NBLK * layer + nb
                    if nb >= 4:
                        pe.wait_ge(table_act, n - 3)
                        pe.wait_ge(table_dve, n - 3)
                    if layer:
                        pe.wait_ge(act_layer, NB * (layer - 1) + nb // 4 + 1)
                    for half in range(2):
                        last = t.matmul(psum[:, 2 * (n % 4) + half, :], source[:, nb * 128:(nb + 1) * 128],
                                        weights[:, half * 4:half * 4 + 4, :].rearrange("p r d -> p (r d)"), start=True, stop=True)
                    last.then_inc(table_mm, 1)
                for c in range(NB):
                    if c == 0:
                        pe.wait_ge(table_act, NBLK * (layer + 1))
                        pe.wait_ge(table_dve, NBLK * (layer + 1))
                    if c >= 8:
                        pe.wait_ge(root_kept, NB * layer + c - 7)
                    t.matmul(psum[:, c % 8, :], root_sb[:, layer, :], source[:, chunk[c]], start=True, stop=True).then_inc(root_mm, 1)

            def conv(k):
                width = D if k < LAYERS else H
                if k < LAYERS:
                    pe.wait_ge(root_kept, NB * (k + 1))
                if k == 0:
                    pe.wait_ge(inv_in, 16)

                def turn_types(i, c):
                    pe.wait_ge(hot_types, NCH * i + c + 1)
                    pe.wait_ge(types_kept, NCH * i + c + 1)
                    for j in range(CH):
                        last = t.matmul(psum[0:3 * R, 6 + c % 2, j * 128:(j + 1) * 128], type_hot[:, c * CH + j, :],
                                        ident16[:, :], start=True, stop=True)
                    last.then_inc(types_turned, 1)

                def spread_weights(i, b, column):
                    pe.wait_ge(types_kept, 2 + NCH * i + b // CH + 1)
                    pe.wait_ge(sel_ready, B * i + b + 1)
                    apart(pe)
                    t.matmul(psum[:, 4 + b % 2, :], type_rows[:, b // CH, (b % CH) * 128:(b % CH + 1) * 128],
                             inv_count[:, bass.ds(column, BW)], start=True, stop=True).then_inc(weight_rows, 1)

                with pe.Fori(0, NIT) as i:
                    if k == 0:
                        turn_types(i, 0)
                        turn_types(i, 1)
                        column = pe.value_load(bucket["dst"][0:1, bass.ds(Q * i, 1)], min_val=0, max_val=NP - BW)
                        spread_weights(i, 0, column)
                        spread_weights(i, 1, column)
                    for b in range(B):
                        if k == 0 and b + 2 < B and b % 2 == 0:
                            column = pe.value_load(bucket["dst"][0:1, bass.ds(Q * i + b // 2 + 1, 1)], min_val=0, max_val=NP - BW)
                        pe.wait_ge(sel_ready, 2 + B * turns(k, i) + b + 1)
                        pe.wait_ge(gathered[b], 16 * (turns(k, i) + 1))
                        if b % 2 == 0:
                            pe.wait_ge(added, Q * turns(k, i) + b // 2 + 1)
                        t.matmul(psum[0:width, b // 2 % PB, :], msg[:, b, 0:width], sel[:, b % SB, :],
                                 start=b % 2 == 0, stop=b % 2 == 1).then_inc(summed, 1)
                        if k == 0:
                            if b % CH == 0 and b // CH + 2 < NCH:
                                turn_types(i, b // CH + 2)
                            if b + 2 < B:
                                spread_weights(i, b + 2, column)

            def moments_of(n):
                for c in range(NB):
                    at = NB * n + c
                    pe.wait_ge(ln_in, at + 1)
                    if c >= 4:
                        pe.wait_ge(ln_centred, at - 3)
                    t.matmul(psum[:, c % 4, :], mean_w[:, :], agg[:, chunk[c]], start=True, stop=True).then_inc(ln_mean, 1)
                for c in range(NB):
                    at = NB * n + c
                    pe.wait_ge(ln_square, at + 1)
                    if c >= 4:
                        pe.wait_ge(ln_std, at - 3)
                    t.matmul(psum[:, 4 + c % 4, :], mean_w[:, :], sel[:, c % 4, :], start=True, stop=True).then_inc(ln_var, 1)

            table(0, xT)
            for layer in range(LAYERS):
                conv(layer)
                if layer < LAYERS - 1:
                    table(layer + 1, cur)
            moments_of(0)
            for c in range(NB):
                pe.wait_ge(ln_out, c + 1)
                if c >= 4:
                    pe.wait_ge(proj_kept, c - 3)
                t.matmul(psum[0:H, c % 4, :], w_in_sb[:, :], xT[:, chunk[c]], start=True, stop=True).then_inc(proj_mm, 1)
            for hop in range(HOPS):
                for m in range(NHB):
                    pe.wait_ge(hop_scaled, NB * hop + min((m + 1) * HB * 128 - 1, NP - 1) // BW + 1)
                    if m == 0:
                        pe.wait_ge(proj_kept, NB)
                    for j in range(HB):
                        nb = m * HB + j
                        last = t.transpose(psum[:, m, j * H:(j + 1) * H], cur[0:H, nb * 128:(nb + 1) * 128], ident[0:H, 0:H])
                    last.then_inc(hop_turned, 1)
                pe.wait_ge(hop_kept, NHB * (hop + 1))
                conv(LAYERS + hop)
            for c in range(NB):
                pe.wait_ge(hop_scaled, NB * HOPS + c + 1)
                if c >= 8:
                    pe.wait_ge(out_biased, c - 7)
                t.matmul(psum[:, c % 8, :], w_out_sb[:, :], bufD[0:H, chunk[c]], start=True, stop=True).then_inc(out_mm, 1)
            pe.wait_ge(out_biased, NB)
            moments_of(1)
            for m in range(NXT):
                pe.wait_ge(ln_out, NB + m + 1)
                if m >= 4:
                    pe.wait_ge(out_kept, m - 3)
                for j, nb in enumerate(blocks_of[m]):
                    last = t.transpose(psum[:, m % 4, j * 128:(j + 1) * 128], xT[:, nb * 128:(nb + 1) * 128], ident[:, :])
                last.then_inc(out_turned, 1)

        @block.vector
        def _(dve):
            v = nc.vector
            steps = [0]

            def link(ins):
                steps[0] += 1
                ins.then_inc(dve_step, 1)
                dve.wait_ge(dve_step, steps[0])

            dve.sem_inc(sel_ready, 2)
            dve.wait_ge(edges_in, 48)
            link(v.scalar_tensor_tensor(out=payload["dst"][:, :, 0], in0=src_i, scalar=float(R), in1=type_i, op0=ALU.mult, op1=ALU.add))
            link(v.tensor_scalar(bucket_i, dst_i, BW.bit_length() - 1, None, ALU.logical_shift_right))
            link(v.scalar_tensor_tensor(out=payload["dst"][:, :, 1], in0=bucket_i, scalar=-float(BW), in1=dst_i, op0=ALU.mult, op1=ALU.add))

            def find_places(k, n):
                for j in range(NB):
                    link(v.tensor_scalar(in_bucket, bucket_i, float(j), None, ALU.is_equal))
                    link(v.tensor_tensor_scan(running, ones[0:EP, 0:1].to_broadcast([EP, EC]), in_bucket, 0.0, ALU.mult, ALU.add))
                    link(v.tensor_copy(hist[:, j:j + 1], running[:, EC - 1:EC]))
                    if j == 0:
                        link(v.tensor_tensor(position, in_bucket, running, ALU.mult))
                    else:
                        link(v.tensor_tensor(term, in_bucket, running, ALU.mult))
                        last = v.tensor_tensor(position, position, term, ALU.add)
                        if j < NB - 1:
                            link(last)
                last.then_inc(hist_ready, 1)
                dve.wait_ge(base_ready, n + 1)
                groups, upto, first, base = (small[0:EP, j, 0:NB] for j in range(4))
                whole, shifted = (small_i[0:EP, j, 0:NB] for j in range(2))
                link(v.tensor_scalar(whole, psum[0:EP, 7, 0:NB], float(GROUP - 1), None, ALU.add))
                link(v.tensor_scalar(shifted, whole, GROUP.bit_length() - 1, None, ALU.logical_shift_right))
                link(v.tensor_copy(groups, shifted))
                link(v.tensor_tensor_scan(upto, ones[0:EP, 0:1].to_broadcast([EP, NB]), groups, 0.0, ALU.mult, ALU.add))
                link(v.tensor_tensor(first, upto, groups, ALU.subtract))
                link(v.scalar_tensor_tensor(out=base, in0=first, scalar=float(GROUP), in1=psum[0:EP, 6, 0:NB], op0=ALU.mult, op1=ALU.add))
                link(v.tensor_scalar(base, base, -1.0, None, ALU.add))
                for j in range(NB):
                    link(v.tensor_scalar(term, bucket_i, float(j), base[:, j:j + 1], ALU.is_equal, ALU.mult))
                    link(v.tensor_tensor(position, position, term, ALU.add))
                pos_i, low_i = in_bucket.bitcast(I32), running.bitcast(I32)
                link(v.tensor_copy(pos_i, position))
                link(v.tensor_scalar(low_i, pos_i, 127, None, ALU.bitwise_and))
                link(v.tensor_scalar(pos_i, pos_i, 7, None, ALU.logical_shift_right))
                link(v.memset(group_f[:, :], 0.0))
                for j in range(NB - 1):
                    link(v.scalar_tensor_tensor(out=group_f[:, :], in0=iota_group[:, :], scalar=upto[0:1, j:j + 1], in1=group_f[:, :],
                                                op0=ALU.is_ge, op1=ALU.add))
                link(v.tensor_scalar(bucket[k][:, :], group_f[:, :], float(BW), None, ALU.mult))
                v.scalar_tensor_tensor(out=address[k][:, :], in0=low_i, scalar=float(NT), in1=pos_i, op0=ALU.mult, op1=ALU.add).then_inc(places_ready, 1)
                dve.wait_ge(places_ready, n + 1)

            dve.wait_ge(constants, CONSTANTS)
            find_places("dst", 0)

            link(v.tensor_scalar(block_i, dst_i, 7, None, ALU.logical_shift_right))
            link(v.scalar_tensor_tensor(out=dst_low, in0=block_i, scalar=-128.0, in1=dst_i, op0=ALU.mult, op1=ALU.add))
            link(v.scalar_tensor_tensor(out=type_block, in0=type_i, scalar=float(NBLK), in1=block_i, op0=ALU.mult, op1=ALU.add))
            link(v.tensor_scalar(block_i, src_i, 7, None, ALU.logical_shift_right))
            link(v.scalar_tensor_tensor(out=src_low, in0=block_i, scalar=-128.0, in1=src_i, op0=ALU.mult, op1=ALU.add))
            link(v.tensor_copy(term, block_i))
            o = R * NBLK

            def hot_turn(i, peeled=False):
                for u in range(CU):
                    if not peeled:
                        dve.wait_ge(counted, CU * i + u + 1 - CU)
                    for at, w, of in ((0, o, type_block), (o, 128, dst_low), (o + 128, NBLK, term), (o + 129 + NBLK, 128, src_low)):
                        last = v.tensor_scalar(hot[:, u, at:at + w], iota16[0:EP, 0:w], of[:, bass.ds(CU * i + u, 1)], None, ALU.is_equal)
                    last.then_inc(hot_ready, 1)
            hot_turn(0, peeled=True)
            with dve.Fori(1, EC // CU) as i:
                hot_turn(i)
            dve.wait_ge(counted, EC + 1)

            link(v.tensor_scalar(bucket_i, src_i, BW.bit_length() - 1, None, ALU.logical_shift_right))
            link(v.scalar_tensor_tensor(out=payload["src"][:, :, 1], in0=bucket_i, scalar=-float(BW), in1=src_i, op0=ALU.mult, op1=ALU.add))
            link(v.tensor_copy(payload["src"][:, :, 0], dst_i))
            find_places("src", 1)

            v.memset(inv_count, 0.0).then_inc(inv_clear, 1)
            dve.wait_ge(inv_clear, 1)
            link(v.tensor_scalar(rest_f, psum[0:CROW, 4, :], 1.0, None, ALU.max))
            link(v.reciprocal(inv_f, rest_f))
            link(v.tensor_copy(inv_parts[:, 0, :], inv_f))
            link(v.tensor_tensor(rest_f, inv_f, inv_parts[:, 0, :], ALU.subtract))
            link(v.tensor_copy(inv_parts[:, 1, :], rest_f))
            v.tensor_tensor(inv_parts[:, 2, :], rest_f, inv_parts[:, 1, :], ALU.subtract).then_inc(inv_ready, 1)
            link(v.tensor_copy(deg_f, psum[0:NBLK, 5, 0:128]))
            v.tensor_scalar(deg_r, deg_f, 1.0, None, ALU.max).then_inc(deg_ready, 1)
            dve.wait_ge(root_ready, 1)
            link(v.reciprocal(deg_r, deg_r))
            v.scalar_tensor_tensor(out=deg_out, in0=deg_f, scalar=0.0, in1=deg_r, op0=ALU.is_gt, op1=ALU.mult).then_inc(deg_done, 1)
            link(v.memset(xT[:, N:NP], 0.0))
            dve.wait_ge(x_kept, NXT)
            link(v.memset(cur[:, N:NP], 0.0))

            def make_weights(layer):
                dve.wait_ge(bases_in, 16 * (layer + 1))
                dve.wait_ge(params_in, 16 * PARAMS)
                if layer:
                    dve.wait_ge(table_mm, NBLK * layer)
                for b in range(BASES):
                    for r in range(R):
                        at = (layer * R + r) * BASES + b
                        factor = comp_sb[:, at:at + 1]
                        if b == 0:
                            last = v.tensor_scalar(weights[:, r, :], bases_sb[:, b, :], factor, None, ALU.mult)
                        else:
                            last = v.scalar_tensor_tensor(out=weights[:, r, :], in0=bases_sb[:, b, :], scalar=factor,
                                                          in1=weights[:, r, :], op0=ALU.mult, op1=ALU.add)
                        if b == BASES - 1 and r == R - 1:
                            last.then_inc(weights_ready, 1)
                        elif r == R - 1 or b == BASES - 1:
                            link(last)

            def table(layer):
                for nb in range(NBLK):
                    n = NBLK * layer + nb
                    dve.wait_ge(table_mm, n + 1)
                    if n >= 4:
                        dve.wait_ge(table_out[n % 4], 16 * (n // 4))
                    v.tensor_copy(table_stage[:, n % 4, 512:1024], psum[:, 2 * (n % 4) + 1, :]).then_inc(table_dve, 1)

            def conv(k):
                width = D if k < LAYERS else H
                which = "dst" if k < LAYERS else "src"
                dve.wait_ge(slots_in, 16 if k < LAYERS else 32)
                if k < LAYERS:
                    for s in range(4):
                        dve.wait_ge(table_out[s], 16 * len(range(s, NBLK * (k + 1), 4)))
                    dve.wait_ge(root_kept, NB * (k + 1))
                else:
                    for m in range(NHB):
                        dve.wait_ge(hop_out[m], 16 * (k - LAYERS + 1))

                def hot_types_of(i, c):
                    dve.wait_ge(types_turned, NCH * i + c + 1)
                    v.tensor_tensor(type_hot[:, c * CH:(c + 1) * CH, :],
                                    type_f[:, bass.ds(B * i + c * CH, CH)].unsqueeze(2).to_broadcast([128, CH, 3 * R]),
                                    iota_types[:, :].unsqueeze(1).to_broadcast([128, CH, 3 * R]), ALU.is_equal).then_inc(hot_types, 1)

                def select(i, b):
                    dve.wait_ge(summed, B + B * turns(k, i) + b + 1 - SB)
                    column = bass.ds(B * i + b, 1)
                    if k == 0:
                        dve.wait_ge(weight_rows, B + B * i + b + 1)
                        ins = v.scalar_tensor_tensor(out=sel[:, b % SB, :], in0=iota[:, :], scalar=slots[:, column, 1],
                                                     in1=psum[:, 4 + b % 2, :], op0=ALU.is_equal, op1=ALU.mult,
                                                     accum_out=norm[:, column])
                    elif k < LAYERS:
                        ins = v.tensor_scalar(sel[:, b % SB, :], iota[:, :], slots[:, column, 1], norm[:, column],
                                              ALU.is_equal, ALU.mult)
                    else:
                        ins = v.tensor_scalar(sel[:, b % SB, :], iota[:, :], slots[:, column, 1], None, ALU.is_equal)
                    ins.then_inc(sel_ready, 1)

                def add(i, q, column):
                    dve.wait_ge(summed, B + B * turns(k, i) + 2 * q + 2)
                    dve.wait_ge(added, PB + Q * turns(k, i) + q)
                    at = agg[0:width, bass.ds(column, BW)]
                    v.tensor_tensor(at, at, psum[0:width, q % PB, :], ALU.add).then_inc(added, 1)

                with dve.Fori(0, NIT) as i:
                    columns = []
                    for q in range(Q):
                        columns.append(dve.value_load(bucket[which][0:1, bass.ds(Q * i + q, 1)], min_val=0, max_val=NP - BW))
                        if k == 0:
                            for c in {0: (0, 1), 1: (2,), 3: (3,)}.get(q, ()):
                                hot_types_of(i, c)
                        select(i, 2 * q)
                        select(i, 2 * q + 1)
                        if q >= 2:
                            add(i, q - 2, columns[q - 2])
                    add(i, Q - 2, columns[Q - 2])
                    add(i, Q - 1, columns[Q - 1])
                dve.wait_ge(added, PB + Q * turns(k + 1, 0))

            def normalise(n, other):
                base = NB * n
                for c in range(NB):
                    if n:
                        dve.wait_ge(out_biased, c + 1)
                    v.tensor_tensor(agg[:, chunk[c]], xT[:, chunk[c]], other[:, chunk[c]], ALU.add).then_inc(ln_in, 1)
                for c in range(NB):
                    dve.wait_ge(ln_mean, base + c + 1)
                    v.tensor_tensor(agg[:, chunk[c]], agg[:, chunk[c]], psum[:, c % 4, :], ALU.subtract).then_inc(ln_centred, 1)
                for c in range(NB):
                    dve.wait_ge(ln_std, base + c + 1)
                    link(v.reciprocal(sel[:, 4 + c % 4, :], sel[:, 4 + c % 4, :]))
                    v.tensor_tensor(xT[:, chunk[c]], agg[:, chunk[c]], sel[:, 4 + c % 4, :], ALU.mult).then_inc(ln_out, 1)

            make_weights(0)
            table(0)
            dve.wait_ge(slots_in, 16)
            link(v.tensor_copy(type_t, slots[:, :, 0]))
            link(v.tensor_scalar(type_t, type_t, R - 1, None, ALU.bitwise_and))
            link(v.tensor_copy(type_f, type_t))
            dve.wait_ge(inv_in, 16)
            for layer in range(LAYERS):
                if layer + 1 < LAYERS:
                    make_weights(layer + 1)
                conv(layer)
                if layer == 0:
                    v.memset(bufE[0:H, NROW:NP], 0.0).then_inc(scale_clear, 1)
                if layer == LAYERS - 1:
                    break
                for c in range(NB):
                    last = v.bn_stats(stats[:, c, :], agg[:, live[c]])
                link(last)
                v.bn_aggr(moments[:, :], stats[:, :, :].rearrange("p c s -> p (c s)")).then_inc(var_ready, 1)
                dve.wait_ge(std_ready, layer + 1)
                link(v.reciprocal(affine[:, 1:2], affine[:, 0:1]))
                link(v.tensor_tensor(affine[:, 2:3], affine[:, 1:2], bn_sb[:, 0, layer:layer + 1], ALU.mult))
                link(v.tensor_tensor(affine[:, 0:1], moments[:, 0:1], affine[:, 2:3], ALU.mult))
                v.tensor_tensor(affine[:, 3:4], bn_sb[:, 1, layer:layer + 1], affine[:, 0:1], ALU.subtract).then_inc(affine_ready, 1)
                table(layer + 1)
            normalise(0, agg)

            dve.wait_ge(scale_in, 16)
            scale, total, hop_cur = bufE[0:H, :], bufD[0:H, :], cur[0:H, :]
            for c in range(NB):
                dve.wait_ge(proj_kept, c + 1)
                link(v.tensor_copy(total[:, chunk[c]], hop_cur[:, chunk[c]]))
                v.tensor_tensor(hop_cur[:, chunk[c]], hop_cur[:, chunk[c]], scale[:, chunk[c]], ALU.mult).then_inc(hop_scaled, 1)
            for hop in range(HOPS):
                link(v.memset(agg[0:H, :], 0.0))
                conv(LAYERS + hop)
                for c in range(NB):
                    link(v.tensor_tensor(hop_cur[:, chunk[c]], agg[0:H, chunk[c]], scale[:, chunk[c]], ALU.mult))
                    last = v.tensor_tensor(total[:, chunk[c]], total[:, chunk[c]], hop_cur[:, chunk[c]], ALU.add)
                    if hop < HOPS - 1:
                        link(last)
                        last = v.tensor_tensor(hop_cur[:, chunk[c]], hop_cur[:, chunk[c]], scale[:, chunk[c]], ALU.mult)
                    last.then_inc(hop_scaled, 1)
            normalise(1, cur)


_INS = ["x", "src", "dst", "edge_type_8", "L0_gnn_bases", "L0_gnn_comp", "L0_gnn_root", "L0_gnn_bias", "L0_gnn_bn_weight",
        "L0_gnn_bn_bias", "L1_gnn_W_in", "L1_gnn_b_in", "L1_gnn_W_out", "L1_gnn_b_out"]


def kernel(**inputs):
    import concourse.bacc as bacc
    from concourse.bass_utils import run_bass_kernel_spmd

    nc = bacc.Bacc("TRN2", target_bir_lowering=False, num_devices=1)
    arrays, args = {}, []
    for name in _INS:
        a = np.ascontiguousarray(inputs[name])
        arrays[f"in_{name}"] = a
        args.append(nc.dram_tensor(f"in_{name}", a.shape, mybir.dt.from_np(a.dtype), kind="ExternalInput").ap())
    args.append(nc.dram_tensor("out", (N, D), F32, kind="ExternalOutput").ap())
    build(nc, *args)
    return run_bass_kernel_spmd(nc, [arrays], core_ids=[0]).results[0]["out"]
```

```python
from contextlib import ExitStack

import numpy as np

import concourse.bass as bass
from concourse import mybir

ALU = mybir.AluOpType
ACT = mybir.ActivationFunctionType
F32 = mybir.dt.float32
F16 = mybir.dt.float16
BF16 = mybir.dt.bfloat16
I32 = mybir.dt.int32

N, E, D, H = 6250, 100000, 128, 64
R, BASES, LAYERS, HOPS = 8, 4, 3, 3
EPS = 1e-5

BW = 512
NB = -(-N // BW)
NP = NB * BW
NBLK = -(-N // 128)
NROW = NBLK * 128
LAST = N - (NBLK - 1) * 128

EP, EC = 125, 800
assert EP * EC == E

B = 16
Q = B // 2
NG = E // 256 + NB
NT = 2 * NG
NIT = -(-NT // B)
LAST_B = NT - B * (NIT - 1)
CH = 4
NCH = B // CH
LAST_CH = -(-LAST_B // CH)
NCHUNK = NCH * (NIT - 1) + LAST_CH
NTP = CH * NCHUNK
WB = 4
HI = BW // 128
TH = R * HI
DC = 6
DCOLS = DC * NIT * LAYERS
SB = 8
PB = 4
GROUP = 2 * 128
NODST = 1048576.0

NPAIR = R // 2
CROW = 2 * NBLK
CU = 16
CU2 = CU // 2
BY_ACT = 5
SU = 16
SH = SU // 2
EMPTY = 2048
RUNB = -(-NT // 128)
NSI = EC // SU
CUTS = (36, 43, NSI)
PAIR = 2048
assert CH == 4 and 128 * (NB - 1) < PAIR
assert LAST_B >= DC and LAST_B % 2 == 0 and DCOLS >= EC
assert R == 2 * NPAIR and EC % CU == 0 and EC % SU == 0


def fills(words):
    parts, at = [], 0
    while at < words:
        p = 128 if words - at >= 256 else (words - at) // 2
        per = min(EMPTY, (words - at) // p // 2 * 2)
        parts.append((at, p, per))
        at += p * per
    return parts


def build(nc, x, src, dst, etype, bases, comp, root, bias, bn_w, bn_b, w_in, b_in, w_out, b_out, out):
    with ExitStack() as ctx:
        def sb(name, shape, dt=F32):
            return ctx.enter_context(nc.sbuf_tensor(name, shape, dt))

        def sem(name):
            return ctx.enter_context(nc.semaphore(name))

        def dram(name, shape, dt=F32):
            return nc.dram_tensor(name, shape, dt).ap()

        msg_table = dram("msg_table", (NROW * R, D))
        hop_table = dram("hop_table", (NROW, H))
        placed = {"dst": dram("placed_dst", (128 * NT + E, 2)), "src": dram("placed_src", (128 * NT, 2))}
        edge_rows = dram("edge_rows", (2 * E, 2))
        inv_count_dram = dram("inv_count", (3 * R * NROW,), BF16)
        inv_sqrt_dram = dram("inv_sqrt", (NROW,))

        xT = sb("xT", [128, NP])
        agg = sb("agg", [128, NP])
        cur = sb("cur", [128, NP])
        bufD = sb("bufD", [128, NP])
        bufE = sb("bufE", [128, NP])
        sel = sb("sel", [128, SB, BW])
        msg = sb("msg", [128, B, D])
        slots = sb("slots", [128, NTP, 2])
        norm = sb("norm", [128, NTP])
        payload = {k: sb(f"payload_{k}", [EP, EC, 2]) for k in ("dst", "src")}
        address = {k: sb(f"address_{k}", [EP, EC]) for k in ("dst", "src")}
        bucket = {k: sb(f"bucket_{k}", [128, NTP // 2], I32) for k in ("dst", "src")}
        bucket_pairs = sb("bucket_pairs", [128, NCHUNK], I32)
        moves = sb("moves", [1, 2, NB], I32)
        unsorted = sb("unsorted", [1, 1], I32)
        next_dst = sb("next_dst", [EP, 2], I32)
        weights = sb("weights", [128, R, D])
        bases_sb = sb("bases_sb", [128, BASES, D])
        comp_sb = sb("comp_sb", [128, LAYERS * R * BASES])
        root_sb = sb("root_sb", [128, LAYERS, D])
        bias_sb = sb("bias_sb", [128, LAYERS])
        bn_sb = sb("bn_sb", [128, 2, LAYERS - 1])
        w_in_sb = sb("w_in_sb", [128, H])
        w_out_sb = sb("w_out_sb", [H, D])
        b_in_sb = sb("b_in_sb", [H, 1])
        b_out_sb = sb("b_out_sb", [128, 1])
        iota = sb("iota", [128, BW])
        iota_types = sb("iota_types", [128, 3 * TH])
        iota16 = sb("iota16", [128, R * NBLK], F16)
        iota_group = sb("iota_group", [128, NTP // 2])
        ident = sb("ident", [128, 128])
        ident16 = sb("ident16", [128, 128], BF16)
        ones = sb("ones", [128, 128])
        mean_w = sb("mean_w", [128, 128])
        earlier = sb("earlier", [128, 128])
        zeros16 = sb("zeros16", [128, BW], F16)
        eps = sb("eps", [128, 1])
        stage_idx = sb("stage_idx", [128, B], I32)
        stage_addr = sb("stage_addr", [EP, SU], I32)
        stage_pay = sb("stage_pay", [EP, SU, 2])
        hist = sb("hist", [EP, NB + 1])
        small = sb("small", [128, 8, 16])
        small_i = sb("small_i", [128, 2, 16], I32)
        group_f = sb("group_f", [128, NTP // 2])
        stats = sb("stats", [128, NB, 6])
        moments = sb("moments", [128, 2])
        affine = sb("affine", [128, 4])

        def part(buf, at, cols, rows=EP, dt=F32):
            v = buf[0:rows, at:at + cols]
            return v if dt is F32 else v.bitcast(dt)

        src_i = part(bufD, 0, EC, dt=I32)
        dst_i = part(bufD, EC, EC, dt=I32)
        type_i = part(bufD, 2 * EC, EC, dt=I32)
        bucket_i = part(bufD, 3 * EC, EC, dt=I32)
        block_i = part(bufD, 4 * EC, EC, dt=I32)
        type_block = part(bufD, 5 * EC, EC)
        dst_low = part(bufD, 6 * EC, EC)
        bucket_f = part(bufD, 7 * EC, EC)
        inv_f = part(bufD, 0, R * NBLK, rows=128)
        rest_f = part(bufD, 512, 512, rows=CROW)
        inv_parts = part(bufD, 1024, 768, rows=CROW, dt=BF16).rearrange("p (a n) -> p a n", a=3)
        src_block = part(bufD, 4 * EC, DCOLS)
        src_low = part(bufD, 4 * EC + DCOLS, DCOLS)
        AT = 4 * EC + 2 * DCOLS
        DHOT = NBLK + 1 + 128
        degree_hot = part(bufD, AT, DC * DHOT // 2, dt=F16).rearrange("p (u n) -> p u n", u=DC)
        AT += DC * DHOT // 2
        deg_f = part(bufD, AT, 128, rows=NBLK)
        deg_r = part(bufD, AT + 128, 128, rows=NBLK)
        deg_out = part(bufD, AT + 256, 128, rows=NBLK)
        late_runs = bufD[:, 0:RUNB * 256].rearrange("p (j e w) -> p j e w", j=RUNB, w=2)

        in_bucket = part(bufE, 0, EC)
        running = part(bufE, EC, EC)
        position = part(bufE, 2 * EC, EC)
        term = part(bufE, 3 * EC, EC)
        HOT = R * NBLK + 128
        hot = part(bufE, 0, CU * HOT // 2, dt=F16).rearrange("p (u n) -> p u n", u=CU)
        away = part(bufE, CU * HOT // 2, CU * 64, dt=F16).rearrange("p (u n) -> p u n", u=CU)
        inv_count = bufE[0:3 * TH, 0:NB * 64].bitcast(BF16)
        inv_count_from = bufE[0:3 * TH, 0:PAIR // 2 + 64].bitcast(BF16)
        AT = NB * 64
        type_rows = bufE[0:3 * TH, AT:AT + WB * CH * 64].bitcast(BF16).rearrange("p (c n) -> p c n", c=WB)
        AT += WB * CH * 64
        type_hot = bufE[:, AT:AT + WB * CH * 3 * TH // 2].bitcast(BF16).rearrange("p (b n) -> p b n", b=WB * CH)
        AT += WB * CH * 3 * TH // 2
        type_f = bufE[:, AT:AT + NTP]
        low_f = bufE[:, AT + NTP:AT + 2 * NTP]
        assert AT + 2 * NTP <= NP
        unread = cur[:, 3 * NTP:3 * NTP + WB * CH * 128].rearrange("p (b n) -> p b n", b=WB * CH)
        type_t = cur[:, 0:NTP].bitcast(I32)
        key_t = cur[:, NTP:2 * NTP].bitcast(I32)
        high_t = cur[:, 2 * NTP:3 * NTP].bitcast(I32)

        rows = cur[:, 0:NROW].rearrange("p (b d) -> p b d", d=D)
        staging = sel[:, :, :].rearrange("p s n -> p (s n)")
        table_stage = staging.rearrange("p (s n) -> p s n", s=4)
        hop_stage = staging.rearrange("p (s n) -> p s n", s=8)
        empty = staging[:, 0:EMPTY].rearrange("p (t w) -> p t w", w=2)
        runs = msg[:, :, :].rearrange("p b d -> p (b d)")[:, 0:RUNB * 256].rearrange("p (j e w) -> p j e w", j=RUNB, w=2)

        psum = ctx.enter_context(nc.psum_tensor("psum", [128, 8, 512], F32))

        edges_in, params_in, rows_in, bases_in = sem("edges_in"), sem("params_in"), sem("rows_in"), sem("bases_in")
        constants = sem("constants")
        dve_step = sem("dve_step")
        empty_set, empty_out = sem("empty_set"), sem("empty_out")
        x_turned, x_kept = sem("x_turned"), sem("x_kept")
        hist_ready, base_ready = sem("hist_ready"), sem("base_ready")
        places_ready = sem("places_ready")
        placing = {k: sem(f"placing_{k}") for k in ("dst", "src")}
        rows_ready, rows_out = sem("rows_ready"), sem("rows_out")
        plan_ready, moved = sem("plan_ready"), sem("moved")
        dst_rank, rank_step = sem("dst_rank"), sem("rank_step")
        dst_placed, runs_in, runs_turned = sem("dst_placed"), sem("runs_in"), sem("runs_turned")
        degree_ready, degrees = sem("degree_ready"), sem("degrees")
        hot_ready, counted = sem("hot_ready"), sem("counted")
        keys_ready, away_ready, low_ready = sem("keys_ready"), sem("away_ready"), sem("low_ready")
        inv_found, inv_turned = sem("inv_found"), sem("inv_turned")
        inv_ready, inv_out, deg_ready, root_ready = sem("inv_ready"), sem("inv_out"), sem("deg_ready"), sem("root_ready")
        deg_done, deg_out_s, inv_clear, inv_in = sem("deg_done"), sem("deg_out_s"), sem("inv_clear"), sem("inv_in")
        scale_clear, scale_in = sem("scale_clear"), sem("scale_in")
        written = {k: [sem(f"written_{k}{h}") for h in range(2)] for k in ("dst", "src")}
        slots_ready = sem("slots_ready")
        weights_ready = sem("weights_ready")
        table_mm, table_act, table_dve = sem("table_mm"), sem("table_act"), sem("table_dve")
        table_out = [sem(f"table_out{s}") for s in range(4)]
        tables_used = sem("tables_used")
        root_mm, root_kept = sem("root_mm"), sem("root_kept")
        staged = sem("staged")
        gathered = [sem(f"gathered{b}") for b in range(B)]
        sel_ready, summed, added = sem("sel_ready"), sem("summed"), sem("added")
        hot_types, types_turned, types_kept, weight_rows, norms = sem("hot_types"), sem("types_turned"), sem("types_kept"), sem("weight_rows"), sem("norms")
        var_ready, std_ready, affine_ready, act_layer = sem("var_ready"), sem("std_ready"), sem("affine_ready"), sem("act_layer")
        ln_in, ln_mean, ln_centred, ln_square = sem("ln_in"), sem("ln_mean"), sem("ln_centred"), sem("ln_square")
        ln_var, ln_std, ln_out = sem("ln_var"), sem("ln_std"), sem("ln_out")
        proj_mm, proj_kept, hop_scaled = sem("proj_mm"), sem("proj_kept"), sem("hop_scaled")
        hop_turned, hop_kept = sem("hop_turned"), sem("hop_kept")
        hop_out = [sem(f"hop_out{s}") for s in range(8)]
        agg_clear = sem("agg_clear")
        out_mm, out_biased = sem("out_mm"), sem("out_biased")
        out_turned, out_kept = sem("out_turned"), sem("out_kept")
        stored = sem("stored")
        passed = sem("passed")

        chunk = [slice(c * BW, (c + 1) * BW) for c in range(NB)]
        live = [slice(c * BW, min((c + 1) * BW, N)) for c in range(NB)]
        NXT = -(-NBLK // 4)
        HB = 7
        assert NBLK % HB == 0
        NHB = NBLK // HB
        CONVS = LAYERS + HOPS
        CONSTANTS = 14
        EMPTIES = ((edge_rows[E:2 * E, :], 2 * E), (placed["src"], 256 * NT), (placed["dst"], 2 * (128 * NT + E)))
        EMPTY_OUT = 16 * sum(len(fills(words)) for _, words in EMPTIES)
        PARAMS = 5 + LAYERS + 2 * (LAYERS - 1)
        blocks_of = [range(4 * m, min(4 * m + 4, NBLK)) for m in range(NXT)]

        def tiles(k, i, b=0):
            return NT * k + B * i + b

        def groups_of(k, i, q=0):
            return NG * k + Q * i + q

        def chunks(k, i, c=0):
            return NCHUNK * k + NCH * i + c

        def gathers(k, i, b):
            return 16 * ((NIT if b < LAST_B else NIT - 1) * k + i + 1)

        def turn_loop(engine, turn):
            with engine.Fori(0, NIT - 1) as i:
                turn(i, B)
            turn(NIT - 1, LAST_B)

        def apart(engine):
            engine.sem_inc(passed, 1)

        block = ctx.enter_context(nc.Block())

        @block.sync
        def _(sp):
            sp.dma_start(bases_sb[:, :, :], bases[0].rearrange("b i o -> i b o")).then_inc(bases_in, 16)
            sp.dma_start(comp_sb[:, :], comp.rearrange("(a l) r b -> a (l r b)", a=1).to_broadcast([128, LAYERS * R * BASES])).then_inc(bases_in, 16)
            sp.dma_start(dst_i, dst.rearrange("(p c) -> p c", p=EP)).then_inc(edges_in, 16)
            sp.dma_start(type_i, etype.rearrange("(p c) -> p c", p=EP)).then_inc(edges_in, 16)
            sp.dma_start(next_dst[0:EP - 1, :], dst[EC:E].rearrange("(p c) -> p c", c=EC)[:, 0:2]).then_inc(edges_in, 16)
            sp.dma_start(src_i, src.rearrange("(p c) -> p c", p=EP)).then_inc(edges_in, 16)
            full = NBLK - 1
            sp.dma_start(rows[:, 0:full, :], x[0:full * 128, :].rearrange("(b p) d -> p b d", p=128)).then_inc(rows_in, 16)
            sp.dma_start(rows[0:LAST, full, :], x[full * 128:N, :]).then_inc(rows_in, 16)
            sp.wait_ge(empty_set, 2)
            for rows_of, words in EMPTIES:
                for at, p, per in fills(words):
                    sp.dma_start(rows_of.rearrange("n w -> (n w)")[at:at + p * per].rearrange("(p n) -> p n", p=p),
                                 staging[0:p, 0:per]).then_inc(empty_out, 16)
            sp.dma_start(root_sb[:, :, :], root.rearrange("l i o -> i l o")).then_inc(params_in, 16)
            for layer in range(LAYERS):
                sp.dma_start(bias_sb[:, layer:layer + 1], bias[layer].rearrange("(o a) -> o a", a=1)).then_inc(params_in, 16)
            for layer in range(LAYERS - 1):
                sp.dma_start(bn_sb[:, 0, layer:layer + 1], bn_w[layer].rearrange("(o a) -> o a", a=1)).then_inc(params_in, 16)
                sp.dma_start(bn_sb[:, 1, layer:layer + 1], bn_b[layer].rearrange("(o a) -> o a", a=1)).then_inc(params_in, 16)
            sp.dma_start(w_in_sb[:, :], w_in).then_inc(params_in, 16)
            sp.dma_start(w_out_sb[:, :], w_out).then_inc(params_in, 16)
            sp.dma_start(b_in_sb[:, :], b_in.rearrange("(p a) -> p a", a=1)).then_inc(params_in, 16)
            sp.dma_start(b_out_sb[:, :], b_out.rearrange("(p a) -> p a", a=1)).then_inc(params_in, 16)
            def table(layer):
                for nb in range(NBLK):
                    n = NBLK * layer + nb
                    sp.wait_ge(table_act, n + 1)
                    if layer:
                        sp.wait_ge(table_dve, NBLK * (layer - 1) + nb + 1)
                    sp.dma_start(msg_table[nb * 128 * R:(nb + 1) * 128 * R, :].rearrange("(p r) d -> p (r d)", r=R),
                                 table_stage[:, n % 4, :]).then_inc(table_out[n % 4], 16)

            def load_runs(k, runs):
                for j in range(RUNB):
                    p = min(128, NT - j * 128)
                    sp.dma_start(runs[0:p, j, :, :].rearrange("p e w -> p (e w)"),
                                 placed[k][j * 128 * 128:(j * 128 + p) * 128, :].rearrange("(p e) w -> p (e w)", p=p)).then_inc(runs_in, 16)

            table(0)
            sp.wait_ge(rows_out, 16)
            sp.wait_ge(plan_ready, 3)
            with sp.If(sp.value_load(unsorted[0:1, 0:1], min_val=0, max_val=1) == 0):
                for j in range(NB):
                    begin = sp.value_load(moves[0:1, 0, j:j + 1], min_val=0, max_val=E)
                    to = sp.value_load(moves[0:1, 1, j:j + 1], min_val=0, max_val=128 * NT)
                    sp.dma_start(placed["dst"][bass.ds(to, E), :].rearrange("(p c) w -> p (c w)", p=EP),
                                  edge_rows[bass.ds(begin, E), :].rearrange("(p c) w -> p (c w)", p=EP)).then_inc(moved, 16)
                    sp.wait_ge(moved, 16 * (j + 1))
                sp.sem_inc(dst_placed, 1)
            sp.wait_ge(dst_placed, 1)
            load_runs("dst", runs)
            sp.wait_ge(inv_ready, 1)
            for a in range(3):
                sp.dma_start(inv_count_dram.rearrange("(a j q n) -> a q j n", a=3, j=NPAIR, q=CROW)[a],
                             inv_parts[:, a, :].rearrange("p (j n) -> p j n", j=NPAIR)).then_inc(inv_out, 16)
            sp.wait_ge(inv_out, 48)
            sp.wait_ge(inv_clear, 1)
            by_type = inv_count_dram.rearrange("(a n) -> a n", a=3 * R)
            full = NBLK // HI
            for h in range(HI):
                sp.dma_start(inv_count[h:3 * TH:HI, 0:full * 128].rearrange("p (b n) -> p b n", n=128),
                             by_type[:, 0:full * BW].rearrange("a (b n) -> a b n", n=BW)[:, :, h * 128:(h + 1) * 128]).then_inc(inv_in, 16)
            sp.dma_start(inv_count[0:3 * TH:HI, full * 128:(full + 1) * 128], by_type[:, full * BW:NROW]).then_inc(inv_in, 16)
            for layer in range(1, LAYERS):
                sp.wait_ge(weights_ready, layer)
                sp.dma_start(bases_sb[:, :, :], bases[layer].rearrange("b i o -> i b o")).then_inc(bases_in, 16)
                table(layer)
            for h in range(2):
                sp.wait_ge(written["src"][h], 16 * SH * NSI)
            load_runs("src", late_runs)
            sp.wait_ge(deg_done, 1)
            sp.dma_start(inv_sqrt_dram.rearrange("(b n) -> b n", b=NBLK), deg_out).then_inc(deg_out_s, 16)
            sp.wait_ge(scale_clear, 1)
            sp.wait_ge(deg_out_s, 16)
            sp.dma_start(bufE[0:H, 0:NROW], inv_sqrt_dram.rearrange("(a n) -> a n", a=1).to_broadcast([H, NROW])).then_inc(scale_in, 16)
            for hop in range(HOPS):
                for m in range(NHB):
                    n = NHB * hop + m
                    sp.wait_ge(hop_kept, n + 1)
                    sp.dma_start(hop_table[m * HB * 128:(m + 1) * HB * 128, :].rearrange("(b p) d -> p b d", p=128),
                                 hop_stage[:, m, 0:HB * H].rearrange("p (b d) -> p b d", d=H)).then_inc(hop_out[m], 16)
            for m in range(NXT):
                sp.wait_ge(out_kept, m + 1)
                bl = blocks_of[m]
                nfull = sum((b + 1) * 128 <= N for b in bl)
                if nfull:
                    sp.dma_start(out[bl[0] * 128:(bl[0] + nfull) * 128, :].rearrange("(b p) d -> p b d", p=128),
                                 cur[:, m * BW:m * BW + nfull * D].rearrange("p (b d) -> p b d", d=D)).then_inc(stored, 16)
                else:
                    sp.dma_start(out[bl[0] * 128:N, :], cur[0:LAST, m * BW:m * BW + D]).then_inc(stored, 16)
            sp.wait_ge(stored, 16 * NXT)

        @block.gpsimd
        def _(pool):
            g = nc.gpsimd
            g.memset(empty[:, :, 0], 0.0).then_inc(empty_set, 1)
            g.memset(empty[:, :, 1], NODST).then_inc(empty_set, 1)
            g.memset(ones[:, :], 1.0).then_inc(constants, 1)
            g.memset(ident[:, :], 0.0).then_inc(constants, 1)
            g.memset(ident16[:, :], 0.0).then_inc(constants, 1)
            g.memset(zeros16[:, :], 0.0).then_inc(constants, 1)
            g.memset(eps[:, :], EPS).then_inc(constants, 1)
            g.memset(mean_w[:, :], 1.0 / D).then_inc(constants, 1)
            g.iota(iota[:, :], [[1, BW]], base=0, channel_multiplier=0, allow_small_or_imprecise_dtypes=True).then_inc(constants, 1)
            g.iota(iota16[:, :], [[1, R * NBLK]], base=0, channel_multiplier=0, allow_small_or_imprecise_dtypes=True).then_inc(constants, 1)
            g.iota(iota_group[:, :], [[1, NTP // 2]], base=0, channel_multiplier=0, allow_small_or_imprecise_dtypes=True).then_inc(constants, 1)
            g.iota(iota_types[:, :], [[0, 3], [1, TH]], base=0, channel_multiplier=0, allow_small_or_imprecise_dtypes=True).then_inc(constants, 1)
            pool.wait_ge(constants, 10)
            for m in (ident, ident16):
                g.affine_select(out=m[:, :], in_=m[:, :], compare_op=ALU.not_equal, fill=1.0, base=0,
                                pattern=[[-1, 128]], channel_multiplier=1).then_inc(constants, 1)
            g.affine_select(out=earlier[:, :], in_=ones[:, :], compare_op=ALU.is_gt, fill=0.0, base=0,
                            pattern=[[1, 128]], channel_multiplier=-1).then_inc(constants, 1)
            g.memset(norm[:, :], 0.0).then_inc(constants, 1)

            def place(k, first, last):
                def turn(i, peeled=False):
                    for h in range(2):
                        if not peeled:
                            pool.wait_ge(written[k][h], 16 * SH * i)
                        here = slice(h * SH, (h + 1) * SH)
                        g.tensor_copy(stage_addr[:, here], address[k][:, bass.ds(SU * i + h * SH, SH)]).then_inc(placing[k], 1)
                        g.tensor_copy(stage_pay[:, here, :], payload[k][:, bass.ds(SU * i + h * SH, SH), :]).then_inc(placing[k], 1)
                        pool.wait_ge(placing[k], 4 * i + 2 * h + 2)
                        apart(pool)
                        for c in range(h * SH, (h + 1) * SH):
                            g.indirect_dma_start(out=placed[k][0:128 * NT, :], out_offset=bass.IndirectOffsetOnAxis(ap=stage_addr[:, c:c + 1], axis=0),
                                                 in_=stage_pay[:, c, :], in_offset=None).then_inc(written[k][h], 16)
                if first == 0:
                    turn(0, peeled=True)
                    first = 1
                with pool.Fori(first, last) as i:
                    turn(i)

            def gather(k):
                table, width = (msg_table, D) if k < LAYERS else (hop_table, H)
                def turn(i, n):
                    for b in range(n):
                        if b % CH == 0:
                            pool.wait_ge(staged, chunks(k, i, b // CH) + 1)
                        pool.wait_ge(summed, tiles(k, i, b) + 1)
                        apart(pool)
                        g.indirect_dma_start(out=msg[:, b, 0:width], out_offset=None, in_=table,
                                             in_offset=bass.IndirectOffsetOnAxis(ap=stage_idx[:, b:b + 1], axis=0)).then_inc(gathered[b], 16)
                turn_loop(pool, turn)

            def squares(n):
                for c in range(NB):
                    at = NB * n + c
                    pool.wait_ge(ln_centred, at + 1)
                    if c >= 4:
                        pool.wait_ge(ln_var, at - 3)
                    g.tensor_tensor(sel[:, c % 4, :], agg[:, chunk[c]], agg[:, chunk[c]], ALU.mult).then_inc(ln_square, 1)

            pool.wait_ge(empty_out, EMPTY_OUT)
            pool.wait_ge(places_ready, 1)
            place("src", 0, CUTS[0])
            pool.wait_ge(plan_ready, 3)
            with pool.If(pool.value_load(unsorted[0:1, 0:1], min_val=0, max_val=1)):
                for h in range(2):
                    pool.wait_ge(written["src"][h], 16 * SH * CUTS[0])
                pool.wait_ge(dst_rank, 1)
                place("dst", 0, NSI)
                for h in range(2):
                    pool.wait_ge(written["dst"][h], 16 * SH * NSI)
                pool.sem_inc(dst_placed, 1)
            for k in range(LAYERS):
                for s in range(4):
                    pool.wait_ge(table_out[s], 16 * len(range(s, NBLK * (k + 1), 4)))
                gather(k)
                if k + 1 < len(CUTS):
                    place("src", CUTS[k], CUTS[k + 1])
            squares(0)
            for hop in range(HOPS):
                for m in range(NHB):
                    pool.wait_ge(hop_out[m], 16 * (hop + 1))
                gather(LAYERS + hop)
            squares(1)

        @block.scalar
        def _(act):
            a = nc.scalar

            def stage(i, c):
                a.copy(stage_idx[:, c * CH:(c + 1) * CH], slots[:, bass.ds(B * i + c * CH, CH), 0]).then_inc(staged, 1)

            def conv(k):
                if k in (0, LAYERS):
                    act.wait_ge(slots_ready, 1 if k == 0 else 2)
                for c in range(NCH):
                    if k:
                        for b in range(c * CH, (c + 1) * CH):
                            act.wait_ge(gathered[b], gathers(k - 1, NIT - 1 if b < LAST_B else NIT - 2, b))
                    stage(0, c)

                def ahead(i, n):
                    for c in range(n):
                        for b in range(c * CH, (c + 1) * CH):
                            act.wait_ge(gathered[b], gathers(k, i, b))
                        stage(i + 1, c)
                with act.Fori(0, NIT - 2) as i:
                    ahead(i, NCH)
                ahead(NIT - 2, LAST_CH)

            def count_low():
                o = R * NBLK
                act.wait_ge(keys_ready, 1)

                def half(i, h, peeled=False):
                    for u in range(CU2 * h, CU2 * h + BY_ACT):
                        last = a.activation(away[:, u, :], iota16[0:EP, 0:128], ACT.Abs, bias=dst_low[:, bass.ds(CU * i + u, 1)], scale=-1.0)
                    last.then_inc(away_ready, 1)
                    act.wait_ge(away_ready, 2 * i + h + 1)
                    if not peeled:
                        act.wait_ge(counted, CU * i + CU2 * h + BY_ACT - CU)
                    a.activation(hot[:, CU2 * h:CU2 * h + BY_ACT, o:o + 128], away[:, CU2 * h:CU2 * h + BY_ACT, :],
                                 ACT.Relu, bias=ones[0:EP, 0:1], scale=-1.0).then_inc(low_ready, 1)
                for h in range(2):
                    half(0, h, peeled=True)
                with act.Fori(1, EC // CU) as i:
                    for h in range(2):
                        half(i, h)

            def keep_types():
                act.sem_inc(types_kept, WB)

                def keep(i, c):
                    act.wait_ge(types_turned, WB + WB * i + c + 1)
                    act.wait_ge(weight_rows, WB * i + c + 1)
                    a.copy(type_rows[:, c, :], psum[0:3 * TH, 4 + c, :]).then_inc(types_kept, 1)
                with act.Fori(0, NCHUNK // WB) as i:
                    for c in range(WB):
                        keep(i, c)
                for c in range(NCHUNK % WB):
                    keep(NCHUNK // WB, c)

            def table(layer):
                for nb in range(NBLK):
                    n = NBLK * layer + nb
                    act.wait_ge(table_mm, n + 1)
                    if n >= 4:
                        act.wait_ge(table_out[n % 4], 16 * (n // 4))
                    if layer == 0:
                        a.copy(table_stage[:, n % 4, 512:1024], psum[:, 2 * (n % 3) + 1, :])
                    a.copy(table_stage[:, n % 4, 0:512], psum[:, 2 * (n % 3), :]).then_inc(table_act, 1)

            def root_part(layer):
                for c in range(NB):
                    act.wait_ge(root_mm, NB * layer + c + 1)
                    a.activation(agg[:, chunk[c]], psum[:, c % 6, :], ACT.Identity, bias=bias_sb[:, layer:layer + 1]).then_inc(root_kept, 1)

            act.wait_ge(params_in, 16 * PARAMS)
            act.wait_ge(constants, CONSTANTS)
            for m in range(NXT):
                act.wait_ge(x_turned, m + 1)
                w = len(blocks_of[m]) * 128 if m < NXT - 1 else LAST
                a.copy(xT[:, m * BW:m * BW + w], psum[:, m % 4, 0:w]).then_inc(x_kept, 1)
            act.wait_ge(empty_out, EMPTY_OUT)
            table(0)
            root_part(0)
            act.wait_ge(rows_ready, 1)
            act.dma_start(edge_rows[0:E, :].rearrange("(p c) w -> p (c w)", p=EP), payload["dst"][:, :, :].rearrange("p c w -> p (c w)")).then_inc(rows_out, 16)
            count_low()
            keep_types()
            for layer in range(LAYERS):
                conv(layer)
                if layer == LAYERS - 1:
                    act.wait_ge(deg_ready, 1)
                    a.activation(deg_r, deg_r, ACT.Sqrt).then_inc(root_ready, 1)
                    break
                act.wait_ge(var_ready, layer + 1)
                a.activation(affine[:, 0:1], moments[:, 1:2], ACT.Sqrt, bias=eps[:, 0:1]).then_inc(std_ready, 1)
                act.wait_ge(affine_ready, layer + 1)
                for c in range(NB):
                    a.activation(cur[:, live[c]], agg[:, live[c]], ACT.Relu, bias=affine[:, 3:4], scale=affine[:, 2:3]).then_inc(act_layer, 1)
                table(layer + 1)
                root_part(layer + 1)

            def deviations(n):
                for c in range(NB):
                    at = NB * n + c
                    act.wait_ge(ln_var, at + 1)
                    if c >= 4:
                        act.wait_ge(ln_out, at - 3)
                    a.activation(sel[:, 4 + c % 4, :], psum[:, 4 + c % 4, :], ACT.Sqrt, bias=eps[:, 0:1]).then_inc(ln_std, 1)

            deviations(0)
            for c in range(NB):
                act.wait_ge(proj_mm, c + 1)
                a.activation(cur[0:H, chunk[c]], psum[0:H, c % 4, :], ACT.Identity, bias=b_in_sb[:, 0:1]).then_inc(proj_kept, 1)
            for hop in range(HOPS):
                for m in range(NHB):
                    act.wait_ge(hop_turned, NHB * hop + m + 1)
                    if hop:
                        act.wait_ge(hop_out[m], 16 * hop)
                    a.copy(hop_stage[:, m, 0:HB * H], psum[:, m, 0:HB * H]).then_inc(hop_kept, 1)
                conv(LAYERS + hop)
            for c in range(NB):
                act.wait_ge(out_mm, c + 1)
                a.activation(cur[:, chunk[c]], psum[:, c % 8, :], ACT.Identity, bias=b_out_sb[:, 0:1], scale=1.0 / (HOPS + 1)).then_inc(out_biased, 1)
            deviations(1)
            for m in range(NXT):
                act.wait_ge(out_turned, m + 1)
                w = len(blocks_of[m]) * D
                a.copy(cur[:, m * BW:m * BW + w], psum[:, m % 4, 0:w]).then_inc(out_kept, 1)

        @block.tensor
        def _(pe):
            t = nc.tensor
            pe.sem_inc(summed, B)
            pe.sem_inc(added, PB)
            pe.sem_inc(types_turned, WB)
            pe.sem_inc(weight_rows, WB)
            pe.sem_inc(degrees, DC)
            pe.wait_ge(constants, CONSTANTS)
            pe.wait_ge(rows_in, 32)
            for m in range(NXT):
                if m >= 4:
                    pe.wait_ge(x_kept, m - 3)
                for j, nb in enumerate(blocks_of[m]):
                    p = 128 if nb < NBLK - 1 else LAST
                    last = t.transpose(psum[:, m % 4, j * 128:j * 128 + p], rows[0:p, nb, :], ident[0:p, 0:p])
                last.then_inc(x_turned, 1)

            def edges_before(n):
                pe.wait_ge(hist_ready, n + 1)
                t.matmul(psum[0:EP, 6, 0:NB], earlier[0:EP, 0:EP], hist[:, 0:NB], start=True, stop=True)
                t.matmul(psum[:, 7, 0:NB + 1], ones[0:EP, :], hist[:, :], start=True, stop=True).then_inc(base_ready, 1)

            def count_types():
                def product(low, high, **flags):
                    return t.matmul(psum[:, 4, 0:R * NBLK], low, high, skip_group_check=True, **flags)
                product(zeros16[0:EP, 0:128], zeros16[0:EP, 0:R * NBLK], start=True, stop=False)
                with pe.Fori(0, EC // CU) as i:
                    for u in range(CU):
                        pe.wait_ge(hot_ready, CU * i + u + 1)
                        if u % CU2 == 0:
                            pe.wait_ge(low_ready, 2 * i + u // CU2 + 1)
                        product(hot[:, u, R * NBLK:R * NBLK + 128], hot[:, u, 0:R * NBLK], start=False, stop=False).then_inc(counted, 1)
                product(zeros16[0:EP, 0:128], zeros16[0:EP, 0:R * NBLK], start=False, stop=True).then_inc(counted, 1)
                pe.wait_ge(inv_found, 1)
                for j in range(NPAIR):
                    last = t.transpose(psum[0:CROW, 5, j * 128:(j + 1) * 128], inv_f[:, j * CROW:(j + 1) * CROW], ident[:, :])
                last.then_inc(inv_turned, 1)

            def edge_weights():
                pe.wait_ge(inv_in, 16 * (HI + 1))

                def turn_types(i, c):
                    pe.wait_ge(hot_types, WB * i + c + 1)
                    pe.wait_ge(types_kept, WB * i + c + 1)
                    for j in range(CH):
                        last = t.matmul(psum[0:3 * TH, 4 + c, j * 128:(j + 1) * 128], type_hot[:, c * CH + j, :],
                                        ident16[:, :], start=True, stop=True)
                    last.then_inc(types_turned, 1)

                def spread_weights(i, c):
                    pair = pe.value_load(bucket_pairs[0:1, bass.ds(WB * i + c, 1)], min_val=0, max_val=PAIR * PAIR - 1)
                    columns = (pair & (PAIR - 1), pair >> (PAIR.bit_length() - 1))
                    pe.wait_ge(types_kept, WB + WB * i + c + 1)
                    pe.wait_ge(norms, WB * i + c + 1)
                    apart(pe)
                    for j in range(CH):
                        last = t.matmul(psum[:, c, j * 128:(j + 1) * 128], type_rows[:, c, j * 128:(j + 1) * 128],
                                        inv_count_from[:, bass.ds(columns[j // 2], 128)], start=True, stop=True)
                    last.then_inc(weight_rows, 1)
                for c in range(WB):
                    turn_types(0, c)
                turns, rest = divmod(NCHUNK, WB)
                with pe.Fori(1, turns) as i:
                    for c in range(WB):
                        spread_weights(i - 1, c)
                        turn_types(i, c)
                for c in range(WB):
                    spread_weights(turns - 1, c)
                    if c < rest:
                        turn_types(turns, c)
                for c in range(rest):
                    spread_weights(turns, c)

            def turn_runs(n, runs):
                pe.wait_ge(runs_in, 16 * RUNB * (n + 1))
                for w in range(2):
                    for j in range(RUNB):
                        p = min(128, NT - j * 128)
                        last = t.transpose(psum[:, 2 * w + j // 4, j % 4 * 128:j % 4 * 128 + p], runs[0:p, j, :, w], ident[0:p, 0:p])
                last.then_inc(runs_turned, 1)

            def table_blocks(layer, source, first, last_block):
                for nb in range(first, last_block):
                    n = NBLK * layer + nb
                    if nb >= 3:
                        pe.wait_ge(table_act, n - 2)
                        if layer:
                            pe.wait_ge(table_dve, n - 2 - NBLK)
                    if layer:
                        pe.wait_ge(act_layer, NB * (layer - 1) + nb // 4 + 1)
                    for half in range(2):
                        last = t.matmul(psum[:, 2 * (n % 3) + half, :], source[:, nb * 128:(nb + 1) * 128],
                                        weights[:, half * 4:half * 4 + 4, :].rearrange("p r d -> p (r d)"), start=True, stop=True)
                    last.then_inc(table_mm, 1)

            def root_product(layer, source):
                pe.wait_ge(table_act, NBLK * (layer + 1))
                if layer:
                    pe.wait_ge(table_dve, NBLK * layer)
                for c in range(NB):
                    if c >= 6:
                        pe.wait_ge(root_kept, NB * layer + c - 5)
                    t.matmul(psum[:, c % 6, :], root_sb[:, layer, :], source[:, chunk[c]], start=True, stop=True).then_inc(root_mm, 1)

            def degree(block, low, **flags):
                return t.matmul(psum[0:NBLK, 7, 0:128], block, low, skip_group_check=True, **flags)

            def conv(k):
                width = D if k < LAYERS else H
                if k < LAYERS:
                    pe.wait_ge(root_kept, NB * (k + 1))

                def turn(i, n):
                    for b in range(n):
                        pe.wait_ge(sel_ready, tiles(k, i, b) + 1)
                        pe.wait_ge(gathered[b], gathers(k, i, b))
                        if b % 2 == 0:
                            pe.wait_ge(added, groups_of(k, i, b // 2) + 1)
                        t.matmul(psum[0:width, b // 2 % PB, :], msg[:, b, 0:width], sel[:, b % SB, :],
                                 start=b % 2 == 0, stop=b % 2 == 1).then_inc(summed, 1)
                        if k < LAYERS and b < DC:
                            pe.wait_ge(degree_ready, DC * (NIT * k + i) + b + 1)
                            u = degree_hot[:, b, :]
                            degree(u[:, 0:NBLK], u[:, NBLK + 1:NBLK + 129], start=False, stop=False).then_inc(degrees, 1)
                turn_loop(pe, turn)

            def moments_of(n):
                for c in range(NB):
                    at = NB * n + c
                    pe.wait_ge(ln_in, at + 1)
                    if c >= 4:
                        pe.wait_ge(ln_centred, at - 3)
                    t.matmul(psum[:, c % 4, :], mean_w[:, :], agg[:, chunk[c]], start=True, stop=True).then_inc(ln_mean, 1)
                for c in range(NB):
                    at = NB * n + c
                    pe.wait_ge(ln_square, at + 1)
                    if c >= 4:
                        pe.wait_ge(ln_std, at - 3)
                    t.matmul(psum[:, 4 + c % 4, :], mean_w[:, :], sel[:, c % 4, :], start=True, stop=True).then_inc(ln_var, 1)

            pe.wait_ge(x_kept, NXT)
            pe.wait_ge(weights_ready, 1)
            table_blocks(0, xT, 0, NBLK // 3)
            edges_before(0)
            table_blocks(0, xT, NBLK // 3, NBLK)
            edges_before(1)
            root_product(0, xT)
            pe.wait_ge(root_kept, NB)
            count_types()
            turn_runs(0, runs)
            pe.wait_ge(slots_ready, 1)
            edge_weights()
            pe.wait_ge(norms, WB + NCHUNK)
            degree(zeros16[0:EP, 0:NBLK], zeros16[0:EP, 0:128], start=True, stop=False)
            for layer in range(LAYERS):
                conv(layer)
                if layer < LAYERS - 1:
                    pe.wait_ge(weights_ready, layer + 2)
                    table_blocks(layer + 1, cur, 0, NBLK)
                    root_product(layer + 1, cur)
            degree(zeros16[0:EP, 0:NBLK], zeros16[0:EP, 0:128], start=False, stop=True).then_inc(degrees, 1)
            pe.wait_ge(added, PB + groups_of(LAYERS, 0))
            turn_runs(1, late_runs)
            pe.wait_ge(slots_ready, 2)
            moments_of(0)
            for c in range(NB):
                pe.wait_ge(ln_out, c + 1)
                if c >= 4:
                    pe.wait_ge(proj_kept, c - 3)
                t.matmul(psum[0:H, c % 4, :], w_in_sb[:, :], xT[:, chunk[c]], start=True, stop=True).then_inc(proj_mm, 1)
            for hop in range(HOPS):
                for m in range(NHB):
                    pe.wait_ge(hop_scaled, NB * hop + min((m + 1) * HB * 128 - 1, NP - 1) // BW + 1)
                    if m == 0:
                        pe.wait_ge(proj_kept, NB)
                    for j in range(HB):
                        nb = m * HB + j
                        last = t.transpose(psum[:, m, j * H:(j + 1) * H], cur[0:H, nb * 128:(nb + 1) * 128], ident[0:H, 0:H])
                    last.then_inc(hop_turned, 1)
                pe.wait_ge(hop_kept, NHB * (hop + 1))
                conv(LAYERS + hop)
            for c in range(NB):
                pe.wait_ge(hop_scaled, NB * HOPS + c + 1)
                if c >= 8:
                    pe.wait_ge(out_biased, c - 7)
                t.matmul(psum[:, c % 8, :], w_out_sb[:, :], bufD[0:H, chunk[c]], start=True, stop=True).then_inc(out_mm, 1)
            pe.wait_ge(out_biased, NB)
            moments_of(1)
            for m in range(NXT):
                pe.wait_ge(ln_out, NB + m + 1)
                if m >= 4:
                    pe.wait_ge(out_kept, m - 3)
                for j, nb in enumerate(blocks_of[m]):
                    last = t.transpose(psum[:, m % 4, j * 128:(j + 1) * 128], xT[:, nb * 128:(nb + 1) * 128], ident[:, :])
                last.then_inc(out_turned, 1)

        @block.vector
        def _(dve):
            v = nc.vector
            steps = [0]

            def link(ins):
                steps[0] += 1
                ins.then_inc(dve_step, 1)
                dve.wait_ge(dve_step, steps[0])

            def make_weights(layer):
                dve.wait_ge(bases_in, 16 * (layer + 2))
                if layer:
                    dve.wait_ge(table_mm, NBLK * layer)
                for b in range(BASES):
                    for r in range(R):
                        at = (layer * R + r) * BASES + b
                        factor = comp_sb[:, at:at + 1]
                        if b == 0:
                            last = v.tensor_scalar(weights[:, r, :], bases_sb[:, b, :], factor, None, ALU.mult)
                        else:
                            last = v.scalar_tensor_tensor(out=weights[:, r, :], in0=bases_sb[:, b, :], scalar=factor,
                                                          in1=weights[:, r, :], op0=ALU.mult, op1=ALU.add)
                        if b == BASES - 1 and r == R - 1:
                            last.then_inc(weights_ready, 1)
                        elif r == R - 1 or b == BASES - 1:
                            link(last)

            dve.sem_inc(norms, WB)
            link(v.memset(xT[:, N:NP], 0.0))
            make_weights(0)
            dve.wait_ge(edges_in, 64)
            link(v.memset(hist[:, :], 0.0))
            dve.wait_ge(constants, CONSTANTS)

            whole, shifted = (small_i[:, j, 0:NB] for j in range(2))
            totals, groups, upto, first, base = (small[:, j, 0:NB] for j in range(5))

            def plan_groups(k, n):
                dve.wait_ge(base_ready, n + 1)
                link(v.tensor_copy(totals, psum[:, 7, 0:NB]))
                link(v.tensor_scalar(whole, totals, float(GROUP - 1), None, ALU.add))
                link(v.tensor_scalar(shifted, whole, GROUP.bit_length() - 1, None, ALU.logical_shift_right))
                link(v.tensor_copy(groups, shifted))
                link(v.tensor_tensor_scan(upto, ones[:, 0:1].to_broadcast([128, NB]), groups, 0.0, ALU.mult, ALU.add))
                link(v.tensor_tensor(first, upto, groups, ALU.subtract))
                link(v.tensor_scalar(first, first, float(GROUP), None, ALU.mult))
                link(v.tensor_tensor(base[0:EP, :], first[0:EP, :], psum[0:EP, 6, 0:NB], ALU.add))
                link(v.tensor_scalar(base[0:EP, :], base[0:EP, :], -1.0, None, ALU.add))
                link(v.memset(group_f[:, :], 0.0))
                for j in range(NB - 1):
                    link(v.scalar_tensor_tensor(out=group_f[:, :], in0=iota_group[:, :], scalar=upto[:, j:j + 1], in1=group_f[:, :],
                                                op0=ALU.is_ge, op1=ALU.add))
                last = v.tensor_scalar(bucket[k][:, :], group_f[:, :], 128.0, None, ALU.mult)
                if k == "dst":
                    link(last)
                    pairs = bucket[k][:, :].rearrange("p (c g) -> p c g", g=2)
                    last = v.scalar_tensor_tensor(out=bucket_pairs[:, :], in0=pairs[:, :, 1], scalar=float(PAIR), in1=pairs[:, :, 0],
                                                  op0=ALU.mult, op1=ALU.add)
                last.then_inc(plan_ready, 1)

            def find_slots(k, step, count=False):
                for j in range(NB):
                    step(v.tensor_scalar(in_bucket, bucket_f, float(j), None, ALU.is_equal))
                    step(v.tensor_tensor_scan(running, ones[0:EP, 0:1].to_broadcast([EP, EC]), in_bucket, 0.0, ALU.mult, ALU.add))
                    if count:
                        step(v.tensor_copy(hist[:, j:j + 1], running[:, EC - 1:EC]))
                    if j == 0:
                        step(v.tensor_tensor(position, in_bucket, running, ALU.mult))
                    else:
                        step(v.tensor_tensor(term, in_bucket, running, ALU.mult))
                        last = v.tensor_tensor(position, position, term, ALU.add)
                        if j < NB - 1 or not count:
                            step(last)
                if count:
                    last.then_inc(hist_ready, 1)
                    plan_groups(k, 0)
                    dve.wait_ge(plan_ready, 1)
                for j in range(NB):
                    step(v.tensor_scalar(term, bucket_f, float(j), base[0:EP, j:j + 1], ALU.is_equal, ALU.mult))
                    if j < NB - 1:
                        step(v.tensor_tensor(position, position, term, ALU.add))
                step(v.tensor_tensor(address[k][:, :], position, term, ALU.add))

            shift = BW.bit_length() - 1
            link(v.tensor_scalar(bucket_i, src_i, shift, None, ALU.logical_shift_right))
            link(v.tensor_copy(bucket_f, bucket_i))
            find_slots("src", link, count=True)
            link(v.tensor_copy(payload["src"][:, :, 1], src_i))
            v.tensor_copy(payload["src"][:, :, 0], dst_i).then_inc(places_ready, 1)

            link(v.tensor_copy(payload["dst"][:, :, 1], dst_i))
            v.scalar_tensor_tensor(out=payload["dst"][:, :, 0], in0=src_i, scalar=float(R), in1=type_i, op0=ALU.mult, op1=ALU.add).then_inc(rows_ready, 1)
            link(v.tensor_scalar(bucket_i, dst_i, shift, None, ALU.logical_shift_right))
            link(v.tensor_copy(bucket_f, bucket_i))
            for j in range(NB):
                link(v.tensor_scalar(in_bucket, bucket_f, float(j), 0.0, ALU.is_equal, ALU.add, accum_out=hist[:, j:j + 1]))
            link(v.memset(term, 0.0))
            link(v.tensor_tensor(term[:, 0:EC - 1], dst_i[:, 0:EC - 1], dst_i[:, 1:EC], ALU.is_gt))
            link(v.tensor_tensor(term[0:EP - 1, EC - 1:EC], dst_i[0:EP - 1, EC - 1:EC], next_dst[0:EP - 1, 0:1], ALU.is_gt))
            v.tensor_reduce(hist[:, NB:NB + 1], term, mybir.AxisListType.X, ALU.add).then_inc(hist_ready, 1)
            plan_groups("dst", 1)
            link(v.tensor_tensor_scan(small[:, 5, 0:NB], ones[:, 0:1].to_broadcast([128, NB]), totals, 0.0, ALU.mult, ALU.add))
            link(v.tensor_tensor(moves[0:1, 0, :], small[0:1, 5, 0:NB], totals[0:1, :], ALU.subtract))
            link(v.tensor_copy(moves[0:1, 1, :], first[0:1, :]))
            v.tensor_scalar(unsorted[:, :], psum[0:1, 7, NB:NB + 1], 0.0, None, ALU.is_gt).then_inc(plan_ready, 1)
            dve.wait_ge(plan_ready, 3)
            with dve.If(dve.value_load(unsorted[0:1, 0:1], min_val=0, max_val=1)):
                ranked = [0]

                def rank_link(ins):
                    ranked[0] += 1
                    ins.then_inc(rank_step, 1)
                    dve.wait_ge(rank_step, ranked[0])
                find_slots("dst", rank_link)
                dve.sem_inc(dst_rank, 1)

            link(v.tensor_scalar(block_i, dst_i, 7, None, ALU.logical_shift_right))
            link(v.scalar_tensor_tensor(out=dst_low, in0=block_i, scalar=-128.0, in1=dst_i, op0=ALU.mult, op1=ALU.add))
            link(v.scalar_tensor_tensor(out=type_block, in0=type_i, scalar=float(NBLK), in1=block_i, op0=ALU.mult, op1=ALU.add))
            dve.sem_inc(keys_ready, 1)
            o = R * NBLK

            def hot_turn(i, peeled=False):
                for u in range(CU):
                    if not peeled:
                        dve.wait_ge(counted, CU * i + u + 1 - CU)
                    last = v.tensor_scalar(hot[:, u, 0:o], iota16[0:EP, 0:o], type_block[:, bass.ds(CU * i + u, 1)], None, ALU.is_equal)
                    if u % CU2 >= BY_ACT:
                        last = v.tensor_scalar(hot[:, u, o:o + 128], iota16[0:EP, 0:128], dst_low[:, bass.ds(CU * i + u, 1)], None, ALU.is_equal)
                    last.then_inc(hot_ready, 1)
            hot_turn(0, peeled=True)
            with dve.Fori(1, EC // CU) as i:
                hot_turn(i)
            dve.wait_ge(counted, EC + 1)

            link(v.memset(src_block, -1.0))
            link(v.memset(src_low, -1.0))
            link(v.tensor_scalar(bucket_i, src_i, 7, None, ALU.logical_shift_right))
            link(v.tensor_copy(src_block[:, 0:EC], bucket_i))
            link(v.scalar_tensor_tensor(out=src_low[:, 0:EC], in0=bucket_i, scalar=-128.0, in1=src_i, op0=ALU.mult, op1=ALU.add))

            link(v.tensor_scalar(inv_f, psum[:, 4, 0:R * NBLK], 1.0, None, ALU.max))
            v.reciprocal(inv_f, inv_f).then_inc(inv_found, 1)
            v.memset(inv_count, 0.0).then_inc(inv_clear, 1)
            dve.wait_ge(inv_turned, 1)
            turned = psum[0:CROW, 5, :]
            link(v.tensor_copy(inv_parts[:, 0, :], turned))
            link(v.tensor_tensor(rest_f, turned, inv_parts[:, 0, :], ALU.subtract))
            link(v.tensor_copy(inv_parts[:, 1, :], rest_f))
            v.tensor_tensor(inv_parts[:, 2, :], rest_f, inv_parts[:, 1, :], ALU.subtract).then_inc(inv_ready, 1)
            dve.wait_ge(x_kept, NXT)
            link(v.memset(cur[:, N:NP], 0.0))

            def keep_slots(k, n):
                dve.wait_ge(runs_turned, n + 1)
                if n == 0:
                    link(v.memset(slots[:, NT:NTP, 0], 0.0))
                    link(v.memset(slots[:, NT:NTP, 1], NODST))
                for h, (lo, hi) in enumerate(((0, BW), (BW, NT))):
                    link(v.tensor_copy(slots[:, lo:hi, 0], psum[:, h, 0:hi - lo]))
                    last = v.scalar_tensor_tensor(out=slots[:, lo:hi, 1].rearrange("p (g t) -> p g t", t=2),
                                                  in0=bucket[k][:, lo // 2:hi // 2].unsqueeze(2).to_broadcast([128, (hi - lo) // 2, 2]),
                                                  scalar=-float(HI), in1=psum[:, 2 + h, 0:hi - lo].rearrange("p (g t) -> p g t", t=2),
                                                  op0=ALU.mult, op1=ALU.add)
                    if h == 0:
                        link(last)
                last.then_inc(slots_ready, 1)
                dve.wait_ge(slots_ready, n + 1)

            def table(layer):
                for nb in range(NBLK):
                    n = NBLK * layer + nb
                    dve.wait_ge(table_mm, n + 1)
                    if n >= 4:
                        dve.wait_ge(table_out[n % 4], 16 * (n // 4))
                    v.tensor_copy(table_stage[:, n % 4, 512:1024], psum[:, 2 * (n % 3) + 1, :]).then_inc(table_dve, 1)

            def conv(k):
                width = D if k < LAYERS else H
                which = "dst" if k < LAYERS else "src"
                if k < LAYERS:
                    for s in range(4):
                        dve.wait_ge(table_out[s], 16 * len(range(s, NBLK * (k + 1), 4)))
                    dve.wait_ge(root_kept, NB * (k + 1))
                else:
                    for m in range(NHB):
                        dve.wait_ge(hop_out[m], 16 * (k - LAYERS + 1))

                def select(i, b):
                    dve.wait_ge(summed, B + tiles(k, i, b) + 1 - SB)
                    column = bass.ds(B * i + b, 1)
                    weight = (norm[:, column], ALU.is_equal, ALU.mult) if k < LAYERS else (None, ALU.is_equal)
                    v.tensor_scalar(sel[:, b % SB, :], iota[:, :], slots[:, column, 1], *weight).then_inc(sel_ready, 1)
                    if k < LAYERS and b < DC:
                        at = DC * (NIT * k + i) + b
                        dve.wait_ge(degrees, at + 1)
                        u = degree_hot[:, b, :]
                        v.tensor_scalar(u[:, 0:NBLK], iota16[0:EP, 0:NBLK], src_block[:, bass.ds(at, 1)], None, ALU.is_equal)
                        v.tensor_scalar(u[:, NBLK + 1:NBLK + 129], iota16[0:EP, 0:128], src_low[:, bass.ds(at, 1)], None,
                                        ALU.is_equal).then_inc(degree_ready, 1)

                def add(i, q, column):
                    dve.wait_ge(summed, B + tiles(k, i) + 2 * q + 2)
                    dve.wait_ge(added, PB + groups_of(k, i, q))
                    at = agg[0:width, bass.ds(column * HI, BW)]
                    v.tensor_tensor(at, at, psum[0:width, q % PB, :], ALU.add).then_inc(added, 1)

                def turn(i, n):
                    columns = []
                    for q in range(n // 2):
                        columns.append(dve.value_load(bucket[which][0:1, bass.ds(Q * i + q, 1)], min_val=0, max_val=(NB - 1) * 128))
                        select(i, 2 * q)
                        select(i, 2 * q + 1)
                        if q >= 2:
                            add(i, q - 2, columns[q - 2])
                    add(i, n // 2 - 2, columns[-2])
                    add(i, n // 2 - 1, columns[-1])
                turn_loop(dve, turn)
                dve.wait_ge(added, PB + groups_of(k + 1, 0))

            def edge_weights():
                def hot_types_of(i, c):
                    dve.wait_ge(types_turned, WB * i + c + 1)
                    v.tensor_tensor(type_hot[:, c * CH:(c + 1) * CH, :],
                                    type_f[:, bass.ds((WB * i + c) * CH, CH)].unsqueeze(2).to_broadcast([128, CH, 3 * TH]),
                                    iota_types[:, :].unsqueeze(1).to_broadcast([128, CH, 3 * TH]), ALU.is_equal).then_inc(hot_types, 1)

                def take(i, c):
                    dve.wait_ge(weight_rows, WB + WB * i + c + 1)
                    dve.wait_ge(norms, WB * i + c + 1)
                    for j in range(CH):
                        at = bass.ds((WB * i + c) * CH + j, 1)
                        last = v.scalar_tensor_tensor(out=unread[:, c * CH + j, :], in0=iota[:, 0:128], scalar=low_f[:, at],
                                                      in1=psum[:, c, j * 128:(j + 1) * 128], op0=ALU.is_equal, op1=ALU.mult,
                                                      accum_out=norm[:, at])
                    last.then_inc(norms, 1)
                for c in range(WB):
                    hot_types_of(0, c)
                turns, rest = divmod(NCHUNK, WB)
                with dve.Fori(1, turns) as i:
                    for c in range(WB):
                        hot_types_of(i, c)
                        take(i - 1, c)
                for c in range(WB):
                    if c < rest:
                        hot_types_of(turns, c)
                    take(turns - 1, c)
                for c in range(rest):
                    take(turns, c)
                dve.wait_ge(norms, WB + NCHUNK)

            def normalise(n, other):
                base = NB * n
                for c in range(NB):
                    if n:
                        dve.wait_ge(out_biased, c + 1)
                    v.tensor_tensor(agg[:, chunk[c]], xT[:, chunk[c]], other[:, chunk[c]], ALU.add).then_inc(ln_in, 1)
                for c in range(NB):
                    dve.wait_ge(ln_mean, base + c + 1)
                    v.tensor_tensor(agg[:, chunk[c]], agg[:, chunk[c]], psum[:, c % 4, :], ALU.subtract).then_inc(ln_centred, 1)
                for c in range(NB):
                    dve.wait_ge(ln_std, base + c + 1)
                    link(v.reciprocal(sel[:, 4 + c % 4, :], sel[:, 4 + c % 4, :]))
                    v.tensor_tensor(xT[:, chunk[c]], agg[:, chunk[c]], sel[:, 4 + c % 4, :], ALU.mult).then_inc(ln_out, 1)

            keep_slots("dst", 0)
            link(v.tensor_copy(type_t, slots[:, :, 0]))
            link(v.tensor_scalar(type_t, type_t, R - 1, None, ALU.bitwise_and))
            link(v.tensor_copy(key_t, slots[:, :, 1]))
            link(v.tensor_scalar(high_t, key_t, 7, None, ALU.logical_shift_right))
            link(v.tensor_scalar(key_t, key_t, 127, None, ALU.bitwise_and))
            link(v.scalar_tensor_tensor(out=type_f, in0=type_t, scalar=float(HI), in1=high_t, op0=ALU.mult, op1=ALU.add))
            link(v.tensor_copy(low_f, key_t))
            edge_weights()
            for layer in range(LAYERS):
                if layer + 1 < LAYERS:
                    make_weights(layer + 1)
                conv(layer)
                if layer == 0:
                    v.memset(bufE[0:H, NROW:NP], 0.0).then_inc(scale_clear, 1)
                if layer == LAYERS - 1:
                    break
                for c in range(NB):
                    last = v.bn_stats(stats[:, c, :], agg[:, live[c]])
                link(last)
                v.bn_aggr(moments[:, :], stats[:, :, :].rearrange("p c s -> p (c s)")).then_inc(var_ready, 1)
                dve.wait_ge(std_ready, layer + 1)
                link(v.reciprocal(affine[:, 1:2], affine[:, 0:1]))
                link(v.tensor_tensor(affine[:, 2:3], affine[:, 1:2], bn_sb[:, 0, layer:layer + 1], ALU.mult))
                link(v.tensor_tensor(affine[:, 0:1], moments[:, 0:1], affine[:, 2:3], ALU.mult))
                v.tensor_tensor(affine[:, 3:4], bn_sb[:, 1, layer:layer + 1], affine[:, 0:1], ALU.subtract).then_inc(affine_ready, 1)
                table(layer + 1)
            dve.wait_ge(degrees, DC + DCOLS + 1)
            link(v.tensor_copy(deg_f, psum[0:NBLK, 7, 0:128]))
            v.tensor_scalar(deg_r, deg_f, 1.0, None, ALU.max).then_inc(deg_ready, 1)
            dve.wait_ge(root_ready, 1)
            link(v.reciprocal(deg_r, deg_r))
            v.scalar_tensor_tensor(out=deg_out, in0=deg_f, scalar=0.0, in1=deg_r, op0=ALU.is_gt, op1=ALU.mult).then_inc(deg_done, 1)
            keep_slots("src", 1)
            normalise(0, agg)

            dve.wait_ge(scale_in, 16)
            scale, total, hop_cur = bufE[0:H, :], bufD[0:H, :], cur[0:H, :]
            for c in range(NB):
                dve.wait_ge(proj_kept, c + 1)
                link(v.tensor_copy(total[:, chunk[c]], hop_cur[:, chunk[c]]))
                v.tensor_tensor(hop_cur[:, chunk[c]], hop_cur[:, chunk[c]], scale[:, chunk[c]], ALU.mult).then_inc(hop_scaled, 1)
            for hop in range(HOPS):
                link(v.memset(agg[0:H, :], 0.0))
                conv(LAYERS + hop)
                for c in range(NB):
                    link(v.tensor_tensor(hop_cur[:, chunk[c]], agg[0:H, chunk[c]], scale[:, chunk[c]], ALU.mult))
                    last = v.tensor_tensor(total[:, chunk[c]], total[:, chunk[c]], hop_cur[:, chunk[c]], ALU.add)
                    if hop < HOPS - 1:
                        link(last)
                        last = v.tensor_tensor(hop_cur[:, chunk[c]], hop_cur[:, chunk[c]], scale[:, chunk[c]], ALU.mult)
                    last.then_inc(hop_scaled, 1)
            normalise(1, cur)


_INS = ["x", "src", "dst", "edge_type_8", "L0_gnn_bases", "L0_gnn_comp", "L0_gnn_root", "L0_gnn_bias", "L0_gnn_bn_weight",
        "L0_gnn_bn_bias", "L1_gnn_W_in", "L1_gnn_b_in", "L1_gnn_W_out", "L1_gnn_b_out"]


def kernel(**inputs):
    import concourse.bacc as bacc
    from concourse.bass_utils import run_bass_kernel_spmd

    nc = bacc.Bacc("TRN2", target_bir_lowering=False, num_devices=1)
    arrays, args = {}, []
    for name in _INS:
        a = np.ascontiguousarray(inputs[name])
        arrays[f"in_{name}"] = a
        args.append(nc.dram_tensor(f"in_{name}", a.shape, mybir.dt.from_np(a.dtype), kind="ExternalInput").ap())
    args.append(nc.dram_tensor("out", (N, D), F32, kind="ExternalOutput").ap())
    build(nc, *args)
    return run_bass_kernel_spmd(nc, [arrays], core_ids=[0]).results[0]["out"]
```

```python
from contextlib import ExitStack

import numpy as np

import concourse.bass as bass
from concourse import mybir

ALU = mybir.AluOpType
ACT = mybir.ActivationFunctionType
F32 = mybir.dt.float32
F16 = mybir.dt.float16
BF16 = mybir.dt.bfloat16
I32 = mybir.dt.int32

N, E, D, H = 6250, 100000, 128, 64
R, BASES, LAYERS, HOPS = 8, 4, 3, 3
EPS = 1e-5

BW = 512
NB = -(-N // BW)
NP = NB * BW
NBLK = -(-N // 128)
NROW = NBLK * 128
LAST = N - (NBLK - 1) * 128

EP, EC = 125, 800
assert EP * EC == E

B = 16
Q = B // 2
NG = E // 256 + NB
NT = 2 * NG
NIT = -(-NT // B)
LAST_B = NT - B * (NIT - 1)
CH = 4
NCH = B // CH
LAST_CH = -(-LAST_B // CH)
NCHUNK = NCH * (NIT - 1) + LAST_CH
NTP = CH * NCHUNK
WB = 4
HI = BW // 128
TH = R * HI
DC = 6
DCOLS = DC * NIT * LAYERS
SB = 8
PB = 4
GROUP = 2 * 128
NODST = 1048576.0

NPAIR = R // 2
CROW = 2 * NBLK
CU = 16
CU2 = CU // 2
BY_ACT = 5
SU = 16
SH = SU // 2
EMPTY = 2048
RUNB = -(-NT // 128)
NSI = EC // SU
CUTS = (38, 44, NSI)
PAIR = 2048
assert CH == 4 and 128 * (NB - 1) < PAIR
assert LAST_B >= DC and LAST_B % 2 == 0 and DCOLS >= EC
assert R == 2 * NPAIR and EC % CU == 0 and EC % SU == 0


def fills(words):
    parts, at = [], 0
    while at < words:
        p = 128 if words - at >= 256 else (words - at) // 2
        per = min(EMPTY, (words - at) // p // 2 * 2)
        parts.append((at, p, per))
        at += p * per
    return parts


def build(nc, x, src, dst, etype, bases, comp, root, bias, bn_w, bn_b, w_in, b_in, w_out, b_out, out):
    with ExitStack() as ctx:
        def sb(name, shape, dt=F32):
            return ctx.enter_context(nc.sbuf_tensor(name, shape, dt))

        def sem(name):
            return ctx.enter_context(nc.semaphore(name))

        def dram(name, shape, dt=F32):
            return nc.dram_tensor(name, shape, dt).ap()

        msg_table = dram("msg_table", (NROW * R, D))
        hop_table = dram("hop_table", (NROW, H))
        placed = {"dst": dram("placed_dst", (128 * NT + E, 2)), "src": dram("placed_src", (128 * NT, 2))}
        edge_rows = dram("edge_rows", (2 * E, 2))
        inv_count_dram = dram("inv_count", (3 * R * NROW,), BF16)
        inv_sqrt_dram = dram("inv_sqrt", (NROW,))

        xT = sb("xT", [128, NP])
        agg = sb("agg", [128, NP])
        cur = sb("cur", [128, NP])
        bufD = sb("bufD", [128, NP])
        bufE = sb("bufE", [128, NP])
        sel = sb("sel", [128, SB, BW])
        msg = sb("msg", [128, B, D])
        slots = sb("slots", [128, NTP, 2])
        norm = sb("norm", [128, NTP])
        payload = {k: sb(f"payload_{k}", [EP, EC, 2]) for k in ("dst", "src")}
        address = {k: sb(f"address_{k}", [EP, EC]) for k in ("dst", "src")}
        bucket = {k: sb(f"bucket_{k}", [128, NTP // 2], I32) for k in ("dst", "src")}
        bucket_pairs = sb("bucket_pairs", [128, NCHUNK], I32)
        moves = sb("moves", [1, 2, NB], I32)
        unsorted = sb("unsorted", [1, 1], I32)
        next_dst = sb("next_dst", [EP, 2], I32)
        weights = sb("weights", [128, R, D])
        bases_sb = sb("bases_sb", [128, BASES, D])
        comp_sb = sb("comp_sb", [128, LAYERS * R * BASES])
        root_sb = sb("root_sb", [128, LAYERS, D])
        bias_sb = sb("bias_sb", [128, LAYERS])
        bn_sb = sb("bn_sb", [128, 2, LAYERS - 1])
        w_in_sb = sb("w_in_sb", [128, 2 * H])
        w_out_sb = sb("w_out_sb", [2 * H, D])
        b_in_sb = sb("b_in_sb", [2 * H, 1])
        b_out_sb = sb("b_out_sb", [128, 1])
        iota = sb("iota", [128, BW])
        iota_types = sb("iota_types", [128, 3 * TH])
        iota16 = sb("iota16", [128, R * NBLK], F16)
        iota_group = sb("iota_group", [128, NTP // 2])
        ident = sb("ident", [128, 128])
        ident16 = sb("ident16", [128, 128], BF16)
        ones = sb("ones", [128, 128])
        earlier = sb("earlier", [128, 128])
        zeros16 = sb("zeros16", [128, BW], F16)
        eps = sb("eps", [128, 1])
        stage_idx = sb("stage_idx", [128, B], I32)
        stage_addr = sb("stage_addr", [EP, SU], I32)
        stage_pay = sb("stage_pay", [EP, SU, 2])
        hist = sb("hist", [EP, NB + 1])
        small = sb("small", [128, 8, 16])
        small_i = sb("small_i", [128, 2, 16], I32)
        group_f = sb("group_f", [128, NTP // 2])
        stats = sb("stats", [128, NB, 6])
        moments = sb("moments", [128, 2])
        affine = sb("affine", [128, 4])
        node_stats = sb("node_stats", [128, 2, HI, 6])
        node_moments = sb("node_moments", [128, NBLK, 2])
        deviation = sb("deviation", [128, NBLK])

        def part(buf, at, cols, rows=EP, dt=F32):
            v = buf[0:rows, at:at + cols]
            return v if dt is F32 else v.bitcast(dt)

        src_i = part(bufD, 0, EC, dt=I32)
        dst_i = part(bufD, EC, EC, dt=I32)
        type_i = part(bufD, 2 * EC, EC, dt=I32)
        bucket_i = part(bufD, 3 * EC, EC, dt=I32)
        block_i = part(bufD, 4 * EC, EC, dt=I32)
        type_block = part(bufD, 5 * EC, EC)
        dst_low = part(bufD, 6 * EC, EC)
        bucket_f = part(bufD, 7 * EC, EC)
        inv_f = part(bufD, 0, R * NBLK, rows=128)
        rest_f = part(bufD, 512, 512, rows=CROW)
        inv_parts = part(bufD, 1024, 768, rows=CROW, dt=BF16).rearrange("p (a n) -> p a n", a=3)
        src_block = part(bufD, 4 * EC, DCOLS)
        src_low = part(bufD, 4 * EC + DCOLS, DCOLS)
        AT = 4 * EC + 2 * DCOLS
        DHOT = NBLK + 1 + 128
        degree_hot = part(bufD, AT, DC * DHOT // 2, dt=F16).rearrange("p (u n) -> p u n", u=DC)
        AT += DC * DHOT // 2
        deg_f = part(bufD, AT, 128, rows=NBLK)
        deg_r = part(bufD, AT + 128, 128, rows=NBLK)
        deg_out = part(bufD, AT + 256, 128, rows=NBLK)
        late_runs = bufD[:, 0:RUNB * 256].rearrange("p (j e w) -> p j e w", j=RUNB, w=2)

        in_bucket = part(bufE, 0, EC)
        running = part(bufE, EC, EC)
        position = part(bufE, 2 * EC, EC)
        term = part(bufE, 3 * EC, EC)
        HOT = R * NBLK + 128
        hot = part(bufE, 0, CU * HOT // 2, dt=F16).rearrange("p (u n) -> p u n", u=CU)
        away = part(bufE, CU * HOT // 2, CU * 64, dt=F16).rearrange("p (u n) -> p u n", u=CU)
        inv_count = bufE[0:3 * TH, 0:NB * 64].bitcast(BF16)
        inv_count_from = bufE[0:3 * TH, 0:PAIR // 2 + 64].bitcast(BF16)
        AT = NB * 64
        type_rows = bufE[0:3 * TH, AT:AT + WB * CH * 64].bitcast(BF16).rearrange("p (c n) -> p c n", c=WB)
        AT += WB * CH * 64
        type_hot = bufE[:, AT:AT + WB * CH * 3 * TH // 2].bitcast(BF16).rearrange("p (b n) -> p b n", b=WB * CH)
        AT += WB * CH * 3 * TH // 2
        type_f = bufE[:, AT:AT + NTP]
        low_f = bufE[:, AT + NTP:AT + 2 * NTP]
        assert AT + 2 * NTP <= NP
        unread = cur[:, 3 * NTP:3 * NTP + WB * CH * 128].rearrange("p (b n) -> p b n", b=WB * CH)
        type_t = cur[:, 0:NTP].bitcast(I32)
        key_t = cur[:, NTP:2 * NTP].bitcast(I32)
        high_t = cur[:, 2 * NTP:3 * NTP].bitcast(I32)

        rows = cur[:, 0:NROW].rearrange("p (b d) -> p b d", d=D)
        staging = sel[:, :, :].rearrange("p s n -> p (s n)")
        table_stage = staging.rearrange("p (s n) -> p s n", s=4)
        hop_stage = staging.rearrange("p (s n) -> p s n", s=8)
        empty = staging[:, 0:EMPTY].rearrange("p (t w) -> p t w", w=2)
        runs = msg[:, :, :].rearrange("p b d -> p (b d)")[:, 0:RUNB * 256].rearrange("p (j e w) -> p j e w", j=RUNB, w=2)

        psum = ctx.enter_context(nc.psum_tensor("psum", [128, 8, 512], F32))

        edges_in, params_in, rows_in, bases_in = sem("edges_in"), sem("params_in"), sem("rows_in"), sem("bases_in")
        constants = sem("constants")
        dve_step = sem("dve_step")
        empty_set, empty_out = sem("empty_set"), sem("empty_out")
        x_turned, x_kept = sem("x_turned"), sem("x_kept")
        hist_ready, base_ready = sem("hist_ready"), sem("base_ready")
        places_ready = sem("places_ready")
        placing = {k: sem(f"placing_{k}") for k in ("dst", "src")}
        rows_ready, rows_out = sem("rows_ready"), sem("rows_out")
        plan_ready, moved = sem("plan_ready"), sem("moved")
        dst_rank, rank_step = sem("dst_rank"), sem("rank_step")
        dst_placed, runs_in, runs_turned = sem("dst_placed"), sem("runs_in"), sem("runs_turned")
        degree_ready, degrees = sem("degree_ready"), sem("degrees")
        hot_ready, counted = sem("hot_ready"), sem("counted")
        keys_ready, away_ready, low_ready = sem("keys_ready"), sem("away_ready"), sem("low_ready")
        inv_found, inv_turned = sem("inv_found"), sem("inv_turned")
        inv_ready, inv_out, deg_ready, root_ready = sem("inv_ready"), sem("inv_out"), sem("deg_ready"), sem("root_ready")
        deg_done, deg_out_s, inv_clear, inv_in = sem("deg_done"), sem("deg_out_s"), sem("inv_clear"), sem("inv_in")
        scale_clear, scale_in = sem("scale_clear"), sem("scale_in")
        written = {k: [sem(f"written_{k}{h}") for h in range(2)] for k in ("dst", "src")}
        slots_ready = sem("slots_ready")
        weights_ready = sem("weights_ready")
        table_mm, table_act, table_dve = sem("table_mm"), sem("table_act"), sem("table_dve")
        table_out = [sem(f"table_out{s}") for s in range(4)]
        root_mm, root_kept = sem("root_mm"), sem("root_kept")
        staged = sem("staged")
        gathered = [sem(f"gathered{b}") for b in range(B)]
        sel_ready, summed, added = sem("sel_ready"), sem("summed"), sem("added")
        hot_types, types_turned, types_kept, weight_rows, norms = sem("hot_types"), sem("types_turned"), sem("types_kept"), sem("weight_rows"), sem("norms")
        var_ready, std_ready, affine_ready, act_layer = sem("var_ready"), sem("std_ready"), sem("affine_ready"), sem("act_layer")
        ln_in, ln_turned, ln_var, ln_std = sem("ln_in"), sem("ln_turned"), sem("ln_var"), sem("ln_std")
        ln_rows, ln_back, ln_out = sem("ln_rows"), sem("ln_back"), sem("ln_out")
        squares_used, first_kept = sem("squares_used"), sem("first_kept")
        proj_mm, proj_kept, hop_scaled = sem("proj_mm"), sem("proj_kept"), sem("hop_scaled")
        hop_turned, hop_kept = sem("hop_turned"), sem("hop_kept")
        hop_out = [sem(f"hop_out{s}") for s in range(8)]
        out_mm, out_biased = sem("out_mm"), sem("out_biased")
        stored = sem("stored")
        passed = sem("passed")

        chunk = [slice(c * BW, (c + 1) * BW) for c in range(NB)]
        live = [slice(c * BW, min((c + 1) * BW, N)) for c in range(NB)]
        NXT = -(-NBLK // 4)
        HB = 7
        assert NBLK % HB == 0
        NHB = NBLK // HB
        CONVS = LAYERS + HOPS
        CONSTANTS = 13
        EMPTIES = ((edge_rows[E:2 * E, :], 2 * E), (placed["src"], 256 * NT), (placed["dst"], 2 * (128 * NT + E)))
        EMPTY_OUT = 16 * sum(len(fills(words)) for _, words in EMPTIES)
        PARAMS = 8 + LAYERS + 2 * (LAYERS - 1)
        blocks_of = [range(4 * m, min(4 * m + 4, NBLK)) for m in range(NXT)]

        def tiles(k, i, b=0):
            return NT * k + B * i + b

        def groups_of(k, i, q=0):
            return NG * k + Q * i + q

        def chunks(k, i, c=0):
            return NCHUNK * k + NCH * i + c

        def gathers(k, i, b):
            return 16 * ((NIT if b < LAST_B else NIT - 1) * k + i + 1)

        def turn_loop(engine, turn):
            with engine.Fori(0, NIT - 1) as i:
                turn(i, B)
            turn(NIT - 1, LAST_B)

        def apart(engine):
            engine.sem_inc(passed, 1)

        block = ctx.enter_context(nc.Block())

        @block.sync
        def _(sp):
            sp.dma_start(bases_sb[:, :, :], bases[0].rearrange("b i o -> i b o")).then_inc(bases_in, 16)
            sp.dma_start(comp_sb[:, :], comp.rearrange("(a l) r b -> a (l r b)", a=1).to_broadcast([128, LAYERS * R * BASES])).then_inc(bases_in, 16)
            sp.dma_start(dst_i, dst.rearrange("(p c) -> p c", p=EP)).then_inc(edges_in, 16)
            sp.dma_start(type_i, etype.rearrange("(p c) -> p c", p=EP)).then_inc(edges_in, 16)
            sp.dma_start(next_dst[0:EP - 1, :], dst[EC:E].rearrange("(p c) -> p c", c=EC)[:, 0:2]).then_inc(edges_in, 16)
            sp.dma_start(src_i, src.rearrange("(p c) -> p c", p=EP)).then_inc(edges_in, 16)
            full = NBLK - 1
            sp.dma_start(rows[:, 0:full, :], x[0:full * 128, :].rearrange("(b p) d -> p b d", p=128)).then_inc(rows_in, 16)
            sp.dma_start(rows[0:LAST, full, :], x[full * 128:N, :]).then_inc(rows_in, 16)
            sp.wait_ge(empty_set, 2)
            for rows_of, words in EMPTIES:
                for at, p, per in fills(words):
                    sp.dma_start(rows_of.rearrange("n w -> (n w)")[at:at + p * per].rearrange("(p n) -> p n", p=p),
                                 staging[0:p, 0:per]).then_inc(empty_out, 16)
            sp.dma_start(root_sb[:, :, :], root.rearrange("l i o -> i l o")).then_inc(params_in, 16)
            for layer in range(LAYERS):
                sp.dma_start(bias_sb[:, layer:layer + 1], bias[layer].rearrange("(o a) -> o a", a=1)).then_inc(params_in, 16)
            for layer in range(LAYERS - 1):
                sp.dma_start(bn_sb[:, 0, layer:layer + 1], bn_w[layer].rearrange("(o a) -> o a", a=1)).then_inc(params_in, 16)
                sp.dma_start(bn_sb[:, 1, layer:layer + 1], bn_b[layer].rearrange("(o a) -> o a", a=1)).then_inc(params_in, 16)
            for half in range(2):
                here = slice(half * H, (half + 1) * H)
                sp.dma_start(w_in_sb[:, here], w_in).then_inc(params_in, 16)
                sp.dma_start(w_out_sb[here, :], w_out).then_inc(params_in, 16)
                sp.dma_start(b_in_sb[here, :], b_in.rearrange("(p a) -> p a", a=1)).then_inc(params_in, 16)
            sp.dma_start(b_out_sb[:, :], b_out.rearrange("(p a) -> p a", a=1)).then_inc(params_in, 16)
            def table(layer):
                for nb in range(NBLK):
                    n = NBLK * layer + nb
                    sp.wait_ge(table_act, n + 1)
                    if layer:
                        sp.wait_ge(table_dve, NBLK * (layer - 1) + nb + 1)
                    sp.dma_start(msg_table[nb * 128 * R:(nb + 1) * 128 * R, :].rearrange("(p r) d -> p (r d)", r=R),
                                 table_stage[:, n % 4, :]).then_inc(table_out[n % 4], 16)

            def load_runs(k, runs):
                for j in range(RUNB):
                    p = min(128, NT - j * 128)
                    sp.dma_start(runs[0:p, j, :, :].rearrange("p e w -> p (e w)"),
                                 placed[k][j * 128 * 128:(j * 128 + p) * 128, :].rearrange("(p e) w -> p (e w)", p=p)).then_inc(runs_in, 16)

            table(0)
            sp.wait_ge(rows_out, 16)
            sp.wait_ge(plan_ready, 3)
            with sp.If(sp.value_load(unsorted[0:1, 0:1], min_val=0, max_val=1) == 0):
                for j in range(NB):
                    begin = sp.value_load(moves[0:1, 0, j:j + 1], min_val=0, max_val=E)
                    to = sp.value_load(moves[0:1, 1, j:j + 1], min_val=0, max_val=128 * NT)
                    sp.dma_start(placed["dst"][bass.ds(to, E), :].rearrange("(p c) w -> p (c w)", p=EP),
                                  edge_rows[bass.ds(begin, E), :].rearrange("(p c) w -> p (c w)", p=EP)).then_inc(moved, 16)
                    sp.wait_ge(moved, 16 * (j + 1))
                sp.sem_inc(dst_placed, 1)
            sp.wait_ge(dst_placed, 1)
            load_runs("dst", runs)
            sp.wait_ge(inv_ready, 1)
            for a in range(3):
                sp.dma_start(inv_count_dram.rearrange("(a j q n) -> a q j n", a=3, j=NPAIR, q=CROW)[a],
                             inv_parts[:, a, :].rearrange("p (j n) -> p j n", j=NPAIR)).then_inc(inv_out, 16)
            sp.wait_ge(inv_out, 48)
            sp.wait_ge(inv_clear, 1)
            by_type = inv_count_dram.rearrange("(a n) -> a n", a=3 * R)
            full = NBLK // HI
            for h in range(HI):
                sp.dma_start(inv_count[h:3 * TH:HI, 0:full * 128].rearrange("p (b n) -> p b n", n=128),
                             by_type[:, 0:full * BW].rearrange("a (b n) -> a b n", n=BW)[:, :, h * 128:(h + 1) * 128]).then_inc(inv_in, 16)
            sp.dma_start(inv_count[0:3 * TH:HI, full * 128:(full + 1) * 128], by_type[:, full * BW:NROW]).then_inc(inv_in, 16)
            for layer in range(1, LAYERS):
                sp.wait_ge(weights_ready, layer)
                sp.dma_start(bases_sb[:, :, :], bases[layer].rearrange("b i o -> i b o")).then_inc(bases_in, 16)
                table(layer)
            for h in range(2):
                sp.wait_ge(written["src"][h], 16 * SH * NSI)
            load_runs("src", late_runs)
            sp.wait_ge(deg_done, 1)
            sp.dma_start(inv_sqrt_dram.rearrange("(b n) -> b n", b=NBLK), deg_out).then_inc(deg_out_s, 16)
            sp.wait_ge(scale_clear, 1)
            sp.wait_ge(deg_out_s, 16)
            def load_scale():
                sp.dma_start(bufE[0:H, 0:NROW], inv_sqrt_dram.rearrange("(a n) -> a n", a=1).to_broadcast([H, NROW])).then_inc(scale_in, 16)
            load_scale()
            for hop in range(HOPS):
                for m in range(NHB):
                    n = NHB * hop + m
                    sp.wait_ge(hop_kept, n + 1)
                    sp.dma_start(hop_table[m * HB * 128:(m + 1) * HB * 128, :].rearrange("(b p) d -> p b d", p=128),
                                 hop_stage[:, m, 0:HB * H].rearrange("p (b d) -> p b d", d=H)).then_inc(hop_out[m], 16)
            sp.wait_ge(squares_used, 1)
            load_scale()
            for m in range(NXT):
                sp.wait_ge(ln_rows, NB + m + 1)
                bl = blocks_of[m]
                nfull = sum((b + 1) * 128 <= N for b in bl)
                if nfull:
                    sp.dma_start(out[bl[0] * 128:(bl[0] + nfull) * 128, :].rearrange("(b p) d -> p b d", p=128),
                                 cur[:, m * BW:m * BW + nfull * D].rearrange("p (b d) -> p b d", d=D)).then_inc(stored, 16)
                else:
                    sp.dma_start(out[bl[0] * 128:N, :], cur[0:LAST, m * BW:m * BW + D]).then_inc(stored, 16)
            sp.wait_ge(stored, 16 * NXT)

        @block.gpsimd
        def _(pool):
            g = nc.gpsimd
            g.memset(empty[:, :, 0], 0.0).then_inc(empty_set, 1)
            g.memset(empty[:, :, 1], NODST).then_inc(empty_set, 1)
            g.memset(ones[:, :], 1.0).then_inc(constants, 1)
            g.memset(ident[:, :], 0.0).then_inc(constants, 1)
            g.memset(ident16[:, :], 0.0).then_inc(constants, 1)
            g.memset(zeros16[:, :], 0.0).then_inc(constants, 1)
            g.memset(eps[:, :], EPS).then_inc(constants, 1)
            g.iota(iota[:, :], [[1, BW]], base=0, channel_multiplier=0, allow_small_or_imprecise_dtypes=True).then_inc(constants, 1)
            g.iota(iota16[:, :], [[1, R * NBLK]], base=0, channel_multiplier=0, allow_small_or_imprecise_dtypes=True).then_inc(constants, 1)
            g.iota(iota_group[:, :], [[1, NTP // 2]], base=0, channel_multiplier=0, allow_small_or_imprecise_dtypes=True).then_inc(constants, 1)
            g.iota(iota_types[:, :], [[0, 3], [1, TH]], base=0, channel_multiplier=0, allow_small_or_imprecise_dtypes=True).then_inc(constants, 1)
            pool.wait_ge(constants, 9)
            for m in (ident, ident16):
                g.affine_select(out=m[:, :], in_=m[:, :], compare_op=ALU.not_equal, fill=1.0, base=0,
                                pattern=[[-1, 128]], channel_multiplier=1).then_inc(constants, 1)
            g.affine_select(out=earlier[:, :], in_=ones[:, :], compare_op=ALU.is_gt, fill=0.0, base=0,
                            pattern=[[1, 128]], channel_multiplier=-1).then_inc(constants, 1)
            g.memset(norm[:, :], 0.0).then_inc(constants, 1)

            def place(k, first, last):
                def turn(i, peeled=False):
                    for h in range(2):
                        if not peeled:
                            pool.wait_ge(written[k][h], 16 * SH * i)
                        here = slice(h * SH, (h + 1) * SH)
                        g.tensor_copy(stage_addr[:, here], address[k][:, bass.ds(SU * i + h * SH, SH)]).then_inc(placing[k], 1)
                        g.tensor_copy(stage_pay[:, here, :], payload[k][:, bass.ds(SU * i + h * SH, SH), :]).then_inc(placing[k], 1)
                        pool.wait_ge(placing[k], 4 * i + 2 * h + 2)
                        apart(pool)
                        for c in range(h * SH, (h + 1) * SH):
                            g.indirect_dma_start(out=placed[k][0:128 * NT, :], out_offset=bass.IndirectOffsetOnAxis(ap=stage_addr[:, c:c + 1], axis=0),
                                                 in_=stage_pay[:, c, :], in_offset=None).then_inc(written[k][h], 16)
                if first == 0:
                    turn(0, peeled=True)
                    first = 1
                with pool.Fori(first, last) as i:
                    turn(i)

            def gather(k):
                table, width = (msg_table, D) if k < LAYERS else (hop_table, H)
                def turn(i, n):
                    for b in range(n):
                        if b % CH == 0:
                            pool.wait_ge(staged, chunks(k, i, b // CH) + 1)
                        pool.wait_ge(summed, tiles(k, i, b) + 1)
                        apart(pool)
                        g.indirect_dma_start(out=msg[:, b, 0:width], out_offset=None, in_=table,
                                             in_offset=bass.IndirectOffsetOnAxis(ap=stage_idx[:, b:b + 1], axis=0)).then_inc(gathered[b], 16)
                turn_loop(pool, turn)

            pool.wait_ge(empty_out, EMPTY_OUT)
            pool.wait_ge(places_ready, 1)
            place("src", 0, CUTS[0])
            pool.wait_ge(plan_ready, 3)
            with pool.If(pool.value_load(unsorted[0:1, 0:1], min_val=0, max_val=1)):
                for h in range(2):
                    pool.wait_ge(written["src"][h], 16 * SH * CUTS[0])
                pool.wait_ge(dst_rank, 1)
                place("dst", 0, NSI)
                for h in range(2):
                    pool.wait_ge(written["dst"][h], 16 * SH * NSI)
                pool.sem_inc(dst_placed, 1)
            for k in range(LAYERS):
                for s in range(4):
                    pool.wait_ge(table_out[s], 16 * len(range(s, NBLK * (k + 1), 4)))
                gather(k)
                if k + 1 < len(CUTS):
                    place("src", CUTS[k], CUTS[k + 1])
            for hop in range(HOPS):
                for m in range(NHB):
                    pool.wait_ge(hop_out[m], 16 * (hop + 1))
                gather(LAYERS + hop)

        @block.scalar
        def _(act):
            a = nc.scalar

            def stage(i, c):
                a.copy(stage_idx[:, c * CH:(c + 1) * CH], slots[:, bass.ds(B * i + c * CH, CH), 0]).then_inc(staged, 1)

            def conv(k):
                if k in (0, LAYERS):
                    act.wait_ge(slots_ready, 1 if k == 0 else 2)
                for c in range(NCH):
                    if k:
                        for b in range(c * CH, (c + 1) * CH):
                            act.wait_ge(gathered[b], gathers(k - 1, NIT - 1 if b < LAST_B else NIT - 2, b))
                    stage(0, c)

                def ahead(i, n):
                    for c in range(n):
                        for b in range(c * CH, (c + 1) * CH):
                            act.wait_ge(gathered[b], gathers(k, i, b))
                        stage(i + 1, c)
                with act.Fori(0, NIT - 2) as i:
                    ahead(i, NCH)
                ahead(NIT - 2, LAST_CH)

            def count_low():
                o = R * NBLK
                act.wait_ge(keys_ready, 1)

                def half(i, h, peeled=False):
                    for u in range(CU2 * h, CU2 * h + BY_ACT):
                        last = a.activation(away[:, u, :], iota16[0:EP, 0:128], ACT.Abs, bias=dst_low[:, bass.ds(CU * i + u, 1)], scale=-1.0)
                    last.then_inc(away_ready, 1)
                    act.wait_ge(away_ready, 2 * i + h + 1)
                    if not peeled:
                        act.wait_ge(counted, CU * i + CU2 * h + BY_ACT - CU)
                    a.activation(hot[:, CU2 * h:CU2 * h + BY_ACT, o:o + 128], away[:, CU2 * h:CU2 * h + BY_ACT, :],
                                 ACT.Relu, bias=ones[0:EP, 0:1], scale=-1.0).then_inc(low_ready, 1)
                for h in range(2):
                    half(0, h, peeled=True)
                with act.Fori(1, EC // CU) as i:
                    for h in range(2):
                        half(i, h)

            def keep_types():
                act.sem_inc(types_kept, WB)

                def keep(i, c):
                    act.wait_ge(types_turned, WB + WB * i + c + 1)
                    act.wait_ge(weight_rows, WB * i + c + 1)
                    a.copy(type_rows[:, c, :], psum[0:3 * TH, 4 + c, :]).then_inc(types_kept, 1)
                with act.Fori(0, NCHUNK // WB) as i:
                    for c in range(WB):
                        keep(i, c)
                for c in range(NCHUNK % WB):
                    keep(NCHUNK // WB, c)

            def table(layer):
                for nb in range(NBLK):
                    n = NBLK * layer + nb
                    act.wait_ge(table_mm, n + 1)
                    if n >= 4:
                        act.wait_ge(table_out[n % 4], 16 * (n // 4))
                    if layer == 0:
                        a.copy(table_stage[:, n % 4, 512:1024], psum[:, 2 * (n % 3) + 1, :])
                    a.copy(table_stage[:, n % 4, 0:512], psum[:, 2 * (n % 3), :]).then_inc(table_act, 1)

            def root_part(layer):
                for c in range(NB):
                    act.wait_ge(root_mm, NB * layer + c + 1)
                    a.activation(agg[:, chunk[c]], psum[:, c % 6, :], ACT.Identity, bias=bias_sb[:, layer:layer + 1]).then_inc(root_kept, 1)

            act.wait_ge(params_in, 16 * PARAMS)
            act.wait_ge(constants, CONSTANTS)
            for m in range(NXT):
                act.wait_ge(x_turned, m + 1)
                w = len(blocks_of[m]) * 128 if m < NXT - 1 else LAST
                a.copy(xT[:, m * BW:m * BW + w], psum[:, m % 4, 0:w]).then_inc(x_kept, 1)
            act.wait_ge(empty_out, EMPTY_OUT)
            table(0)
            root_part(0)
            act.wait_ge(rows_ready, 1)
            act.dma_start(edge_rows[0:E, :].rearrange("(p c) w -> p (c w)", p=EP), payload["dst"][:, :, :].rearrange("p c w -> p (c w)")).then_inc(rows_out, 16)
            count_low()
            keep_types()
            for layer in range(LAYERS):
                conv(layer)
                if layer == LAYERS - 1:
                    act.wait_ge(deg_ready, 1)
                    a.activation(deg_r, deg_r, ACT.Sqrt).then_inc(root_ready, 1)
                    break
                act.wait_ge(var_ready, layer + 1)
                a.activation(affine[:, 0:1], moments[:, 1:2], ACT.Sqrt, bias=eps[:, 0:1]).then_inc(std_ready, 1)
                act.wait_ge(affine_ready, layer + 1)
                for c in range(NB):
                    a.activation(cur[:, live[c]], agg[:, live[c]], ACT.Relu, bias=affine[:, 3:4], scale=affine[:, 2:3]).then_inc(act_layer, 1)
                table(layer + 1)
                root_part(layer + 1)

            def deviations(n, c):
                act.wait_ge(ln_var, NB * n + c + 1)
                bl = blocks_of[c]
                here = slice(bl[0], bl[-1] + 1)
                a.activation(deviation[:, here], node_moments[:, here, 1], ACT.Sqrt, bias=eps[:, 0:1]).then_inc(ln_std, 1)

            act.wait_ge(deg_out_s, 16)
            for c in range(NB + 3):
                if c < NB:
                    deviations(0, c)
                if 2 <= c < NB + 2:
                    act.wait_ge(ln_back, c - 1)
                    at, w = (c - 2) * BW, len(blocks_of[c - 2]) * 128
                    a.copy(xT[:, at:at + w], psum[:, 4 + c % 2, 0:w]).then_inc(ln_out, 1)
                if c >= 3:
                    at = c - 3
                    act.wait_ge(proj_mm, at + 1)
                    a.activation(cur[0:H, chunk[at]], psum[0:H, 6 + at % 2, :], ACT.Identity, bias=b_in_sb[0:H, 0:1]).then_inc(proj_kept, 1)
                    a.activation(bufD[H:2 * H, chunk[at]], psum[H:2 * H, 6 + at % 2, :], ACT.Identity, bias=b_in_sb[H:2 * H, 0:1]).then_inc(first_kept, 1)
            for hop in range(HOPS):
                for m in range(NHB):
                    act.wait_ge(hop_turned, NHB * hop + m + 1)
                    if hop:
                        act.wait_ge(hop_out[m], 16 * hop)
                    a.copy(hop_stage[:, m, 0:HB * H], psum[:, m, 0:HB * H]).then_inc(hop_kept, 1)
                conv(LAYERS + hop)
            for c in range(NB):
                act.wait_ge(out_mm, c + 1)
                a.activation(cur[:, chunk[c]], psum[:, c % 8, :], ACT.Identity, bias=b_out_sb[:, 0:1], scale=1.0 / (HOPS + 1)).then_inc(out_biased, 1)
            for c in range(NB):
                deviations(1, c)

        @block.tensor
        def _(pe):
            t = nc.tensor
            pe.sem_inc(summed, B)
            pe.sem_inc(added, PB)
            pe.sem_inc(types_turned, WB)
            pe.sem_inc(weight_rows, WB)
            pe.sem_inc(degrees, DC)
            pe.wait_ge(constants, CONSTANTS)
            pe.wait_ge(rows_in, 32)
            for m in range(NXT):
                if m >= 4:
                    pe.wait_ge(x_kept, m - 3)
                for j, nb in enumerate(blocks_of[m]):
                    p = 128 if nb < NBLK - 1 else LAST
                    last = t.transpose(psum[:, m % 4, j * 128:j * 128 + p], rows[0:p, nb, :], ident[0:p, 0:p])
                last.then_inc(x_turned, 1)

            def edges_before(n):
                pe.wait_ge(hist_ready, n + 1)
                t.matmul(psum[0:EP, 6, 0:NB], earlier[0:EP, 0:EP], hist[:, 0:NB], start=True, stop=True)
                t.matmul(psum[:, 7, 0:NB + 1], ones[0:EP, :], hist[:, :], start=True, stop=True).then_inc(base_ready, 1)

            def count_types():
                def product(low, high, **flags):
                    return t.matmul(psum[:, 4, 0:R * NBLK], low, high, skip_group_check=True, **flags)
                product(zeros16[0:EP, 0:128], zeros16[0:EP, 0:R * NBLK], start=True, stop=False)
                with pe.Fori(0, EC // CU) as i:
                    for u in range(CU):
                        pe.wait_ge(hot_ready, CU * i + u + 1)
                        if u % CU2 == 0:
                            pe.wait_ge(low_ready, 2 * i + u // CU2 + 1)
                        product(hot[:, u, R * NBLK:R * NBLK + 128], hot[:, u, 0:R * NBLK], start=False, stop=False).then_inc(counted, 1)
                product(zeros16[0:EP, 0:128], zeros16[0:EP, 0:R * NBLK], start=False, stop=True).then_inc(counted, 1)
                pe.wait_ge(inv_found, 1)
                for j in range(NPAIR):
                    last = t.transpose(psum[0:CROW, 5, j * 128:(j + 1) * 128], inv_f[:, j * CROW:(j + 1) * CROW], ident[:, :])
                last.then_inc(inv_turned, 1)

            def edge_weights():
                pe.wait_ge(inv_in, 16 * (HI + 1))

                def turn_types(i, c):
                    pe.wait_ge(hot_types, WB * i + c + 1)
                    pe.wait_ge(types_kept, WB * i + c + 1)
                    for j in range(CH):
                        last = t.matmul(psum[0:3 * TH, 4 + c, j * 128:(j + 1) * 128], type_hot[:, c * CH + j, :],
                                        ident16[:, :], start=True, stop=True)
                    last.then_inc(types_turned, 1)

                def spread_weights(i, c):
                    pair = pe.value_load(bucket_pairs[0:1, bass.ds(WB * i + c, 1)], min_val=0, max_val=PAIR * PAIR - 1)
                    columns = (pair & (PAIR - 1), pair >> (PAIR.bit_length() - 1))
                    pe.wait_ge(types_kept, WB + WB * i + c + 1)
                    pe.wait_ge(norms, WB * i + c + 1)
                    apart(pe)
                    for j in range(CH):
                        last = t.matmul(psum[:, c, j * 128:(j + 1) * 128], type_rows[:, c, j * 128:(j + 1) * 128],
                                        inv_count_from[:, bass.ds(columns[j // 2], 128)], start=True, stop=True)
                    last.then_inc(weight_rows, 1)
                for c in range(WB):
                    turn_types(0, c)
                turns, rest = divmod(NCHUNK, WB)
                with pe.Fori(1, turns) as i:
                    for c in range(WB):
                        spread_weights(i - 1, c)
                        turn_types(i, c)
                for c in range(WB):
                    spread_weights(turns - 1, c)
                    if c < rest:
                        turn_types(turns, c)
                for c in range(rest):
                    spread_weights(turns, c)

            def turn_runs(n, runs):
                pe.wait_ge(runs_in, 16 * RUNB * (n + 1))
                for w in range(2):
                    for j in range(RUNB):
                        p = min(128, NT - j * 128)
                        last = t.transpose(psum[:, 2 * w + j // 4, j % 4 * 128:j % 4 * 128 + p], runs[0:p, j, :, w], ident[0:p, 0:p])
                last.then_inc(runs_turned, 1)

            def table_blocks(layer, source, first, last_block):
                for nb in range(first, last_block):
                    n = NBLK * layer + nb
                    if nb >= 3:
                        pe.wait_ge(table_act, n - 2)
                        if layer:
                            pe.wait_ge(table_dve, n - 2 - NBLK)
                    if layer:
                        pe.wait_ge(act_layer, NB * (layer - 1) + nb // 4 + 1)
                    for half in range(2):
                        last = t.matmul(psum[:, 2 * (n % 3) + half, :], source[:, nb * 128:(nb + 1) * 128],
                                        weights[:, half * 4:half * 4 + 4, :].rearrange("p r d -> p (r d)"), start=True, stop=True)
                    last.then_inc(table_mm, 1)

            def root_product(layer, source):
                pe.wait_ge(table_act, NBLK * (layer + 1))
                if layer:
                    pe.wait_ge(table_dve, NBLK * layer)
                for c in range(NB):
                    if c >= 6:
                        pe.wait_ge(root_kept, NB * layer + c - 5)
                    t.matmul(psum[:, c % 6, :], root_sb[:, layer, :], source[:, chunk[c]], start=True, stop=True).then_inc(root_mm, 1)

            def degree(block, low, **flags):
                return t.matmul(psum[0:NBLK, 7, 0:128], block, low, skip_group_check=True, **flags)

            def conv(k):
                width = D if k < LAYERS else H
                if k < LAYERS:
                    pe.wait_ge(root_kept, NB * (k + 1))

                def turn(i, n):
                    for b in range(n):
                        pe.wait_ge(sel_ready, tiles(k, i, b) + 1)
                        pe.wait_ge(gathered[b], gathers(k, i, b))
                        if b % 2 == 0:
                            pe.wait_ge(added, groups_of(k, i, b // 2) + 1)
                        t.matmul(psum[0:width, b // 2 % PB, :], msg[:, b, 0:width], sel[:, b % SB, :],
                                 start=b % 2 == 0, stop=b % 2 == 1).then_inc(summed, 1)
                        if k < LAYERS and b < DC:
                            pe.wait_ge(degree_ready, DC * (NIT * k + i) + b + 1)
                            u = degree_hot[:, b, :]
                            degree(u[:, 0:NBLK], u[:, NBLK + 1:NBLK + 129], start=False, stop=False).then_inc(degrees, 1)
                turn_loop(pe, turn)

            def turn_rows(n, c):
                pe.wait_ge(ln_in, NB * n + c + 1)
                if c >= 4:
                    pe.wait_ge(ln_rows, NB * n + c - 3)
                for j, nb in enumerate(blocks_of[c]):
                    last = t.transpose(psum[:, c % 4, j * 128:(j + 1) * 128], agg[:, nb * 128:(nb + 1) * 128], ident[:, :])
                last.then_inc(ln_turned, 1)

            def turn_back(c):
                pe.wait_ge(ln_rows, c + 1)
                if c >= 2:
                    pe.wait_ge(ln_out, c - 1)
                for j in range(len(blocks_of[c])):
                    last = t.transpose(psum[:, 4 + c % 2, j * 128:(j + 1) * 128], sel[:, c % 4, j * 128:(j + 1) * 128], ident[:, :])
                last.then_inc(ln_back, 1)

            def project(c):
                pe.wait_ge(ln_out, c + 1)
                if c >= 2:
                    pe.wait_ge(first_kept, c - 1)
                t.matmul(psum[:, 6 + c % 2, :], w_in_sb[:, :], xT[:, chunk[c]], start=True, stop=True).then_inc(proj_mm, 1)

            pe.wait_ge(x_kept, NXT)
            pe.wait_ge(weights_ready, 1)
            table_blocks(0, xT, 0, NBLK // 3)
            edges_before(0)
            table_blocks(0, xT, NBLK // 3, NBLK)
            edges_before(1)
            root_product(0, xT)
            pe.wait_ge(root_kept, NB)
            count_types()
            turn_runs(0, runs)
            pe.wait_ge(slots_ready, 1)
            edge_weights()
            pe.wait_ge(norms, WB + NCHUNK)
            degree(zeros16[0:EP, 0:NBLK], zeros16[0:EP, 0:128], start=True, stop=False)
            for layer in range(LAYERS):
                conv(layer)
                if layer < LAYERS - 1:
                    pe.wait_ge(weights_ready, layer + 2)
                    table_blocks(layer + 1, cur, 0, NBLK)
                    root_product(layer + 1, cur)
            degree(zeros16[0:EP, 0:NBLK], zeros16[0:EP, 0:128], start=False, stop=True).then_inc(degrees, 1)
            pe.wait_ge(added, PB + groups_of(LAYERS, 0))
            turn_runs(1, late_runs)
            pe.wait_ge(slots_ready, 2)
            for c in range(NB + 3):
                if c < NB:
                    turn_rows(0, c)
                if 2 <= c < NB + 2:
                    turn_back(c - 2)
                if c >= 3:
                    project(c - 3)
            for hop in range(HOPS):
                for m in range(NHB):
                    pe.wait_ge(hop_scaled, NB * hop + min((m + 1) * HB * 128 - 1, NP - 1) // BW + 1)
                    if hop == 0 and m == 0:
                        pe.wait_ge(first_kept, NB)
                    for j in range(HB):
                        nb = m * HB + j
                        last = t.transpose(psum[:, m, j * H:(j + 1) * H], cur[0:H, nb * 128:(nb + 1) * 128], ident[0:H, 0:H])
                    last.then_inc(hop_turned, 1)
                pe.wait_ge(hop_kept, NHB * (hop + 1))
                conv(LAYERS + hop)
            for c in range(NB):
                pe.wait_ge(hop_scaled, NB * HOPS + c + 1)
                if c >= 8:
                    pe.wait_ge(out_biased, c - 7)
                t.matmul(psum[:, c % 8, :], w_out_sb[:, :], bufD[:, chunk[c]], start=True, stop=True).then_inc(out_mm, 1)
            pe.wait_ge(out_biased, NB)
            for c in range(NB):
                turn_rows(1, c)

        @block.vector
        def _(dve):
            v = nc.vector
            steps = [0]

            def link(ins):
                steps[0] += 1
                ins.then_inc(dve_step, 1)
                dve.wait_ge(dve_step, steps[0])

            def make_weights(layer):
                dve.wait_ge(bases_in, 16 * (layer + 2))
                if layer:
                    dve.wait_ge(table_mm, NBLK * layer)
                for b in range(BASES):
                    for r in range(R):
                        at = (layer * R + r) * BASES + b
                        factor = comp_sb[:, at:at + 1]
                        if b == 0:
                            last = v.tensor_scalar(weights[:, r, :], bases_sb[:, b, :], factor, None, ALU.mult)
                        else:
                            last = v.scalar_tensor_tensor(out=weights[:, r, :], in0=bases_sb[:, b, :], scalar=factor,
                                                          in1=weights[:, r, :], op0=ALU.mult, op1=ALU.add)
                        if b == BASES - 1 and r == R - 1:
                            last.then_inc(weights_ready, 1)
                        elif r == R - 1 or b == BASES - 1:
                            link(last)

            dve.sem_inc(norms, WB)
            link(v.memset(xT[:, N:NP], 0.0))
            make_weights(0)
            dve.wait_ge(edges_in, 64)
            link(v.memset(hist[:, :], 0.0))
            dve.wait_ge(constants, CONSTANTS)

            whole, shifted = (small_i[:, j, 0:NB] for j in range(2))
            totals, groups, upto, first, base = (small[:, j, 0:NB] for j in range(5))

            def plan_groups(k, n):
                dve.wait_ge(base_ready, n + 1)
                link(v.tensor_copy(totals, psum[:, 7, 0:NB]))
                link(v.tensor_scalar(whole, totals, float(GROUP - 1), None, ALU.add))
                link(v.tensor_scalar(shifted, whole, GROUP.bit_length() - 1, None, ALU.logical_shift_right))
                link(v.tensor_copy(groups, shifted))
                link(v.tensor_tensor_scan(upto, ones[:, 0:1].to_broadcast([128, NB]), groups, 0.0, ALU.mult, ALU.add))
                link(v.tensor_tensor(first, upto, groups, ALU.subtract))
                link(v.tensor_scalar(first, first, float(GROUP), None, ALU.mult))
                link(v.tensor_tensor(base[0:EP, :], first[0:EP, :], psum[0:EP, 6, 0:NB], ALU.add))
                link(v.tensor_scalar(base[0:EP, :], base[0:EP, :], -1.0, None, ALU.add))
                link(v.memset(group_f[:, :], 0.0))
                for j in range(NB - 1):
                    link(v.scalar_tensor_tensor(out=group_f[:, :], in0=iota_group[:, :], scalar=upto[:, j:j + 1], in1=group_f[:, :],
                                                op0=ALU.is_ge, op1=ALU.add))
                last = v.tensor_scalar(bucket[k][:, :], group_f[:, :], 128.0, None, ALU.mult)
                if k == "dst":
                    link(last)
                    pairs = bucket[k][:, :].rearrange("p (c g) -> p c g", g=2)
                    last = v.scalar_tensor_tensor(out=bucket_pairs[:, :], in0=pairs[:, :, 1], scalar=float(PAIR), in1=pairs[:, :, 0],
                                                  op0=ALU.mult, op1=ALU.add)
                last.then_inc(plan_ready, 1)

            def find_slots(k, step, count=False):
                for j in range(NB):
                    step(v.tensor_scalar(in_bucket, bucket_f, float(j), None, ALU.is_equal))
                    step(v.tensor_tensor_scan(running, ones[0:EP, 0:1].to_broadcast([EP, EC]), in_bucket, 0.0, ALU.mult, ALU.add))
                    if count:
                        step(v.tensor_copy(hist[:, j:j + 1], running[:, EC - 1:EC]))
                    if j == 0:
                        step(v.tensor_tensor(position, in_bucket, running, ALU.mult))
                    else:
                        step(v.tensor_tensor(term, in_bucket, running, ALU.mult))
                        last = v.tensor_tensor(position, position, term, ALU.add)
                        if j < NB - 1 or not count:
                            step(last)
                if count:
                    last.then_inc(hist_ready, 1)
                    plan_groups(k, 0)
                    dve.wait_ge(plan_ready, 1)
                for j in range(NB):
                    step(v.tensor_scalar(term, bucket_f, float(j), base[0:EP, j:j + 1], ALU.is_equal, ALU.mult))
                    if j < NB - 1:
                        step(v.tensor_tensor(position, position, term, ALU.add))
                step(v.tensor_tensor(address[k][:, :], position, term, ALU.add))

            shift = BW.bit_length() - 1
            link(v.tensor_scalar(bucket_i, src_i, shift, None, ALU.logical_shift_right))
            link(v.tensor_copy(bucket_f, bucket_i))
            find_slots("src", link, count=True)
            link(v.tensor_copy(payload["src"][:, :, 1], src_i))
            v.tensor_copy(payload["src"][:, :, 0], dst_i).then_inc(places_ready, 1)

            link(v.tensor_copy(payload["dst"][:, :, 1], dst_i))
            v.scalar_tensor_tensor(out=payload["dst"][:, :, 0], in0=src_i, scalar=float(R), in1=type_i, op0=ALU.mult, op1=ALU.add).then_inc(rows_ready, 1)
            link(v.tensor_scalar(bucket_i, dst_i, shift, None, ALU.logical_shift_right))
            link(v.tensor_copy(bucket_f, bucket_i))
            for j in range(NB):
                link(v.tensor_scalar(in_bucket, bucket_f, float(j), 0.0, ALU.is_equal, ALU.add, accum_out=hist[:, j:j + 1]))
            link(v.memset(term, 0.0))
            link(v.tensor_tensor(term[:, 0:EC - 1], dst_i[:, 0:EC - 1], dst_i[:, 1:EC], ALU.is_gt))
            link(v.tensor_tensor(term[0:EP - 1, EC - 1:EC], dst_i[0:EP - 1, EC - 1:EC], next_dst[0:EP - 1, 0:1], ALU.is_gt))
            v.tensor_reduce(hist[:, NB:NB + 1], term, mybir.AxisListType.X, ALU.add).then_inc(hist_ready, 1)
            plan_groups("dst", 1)
            link(v.tensor_tensor_scan(small[:, 5, 0:NB], ones[:, 0:1].to_broadcast([128, NB]), totals, 0.0, ALU.mult, ALU.add))
            link(v.tensor_tensor(moves[0:1, 0, :], small[0:1, 5, 0:NB], totals[0:1, :], ALU.subtract))
            link(v.tensor_copy(moves[0:1, 1, :], first[0:1, :]))
            v.tensor_scalar(unsorted[:, :], psum[0:1, 7, NB:NB + 1], 0.0, None, ALU.is_gt).then_inc(plan_ready, 1)
            dve.wait_ge(plan_ready, 3)
            with dve.If(dve.value_load(unsorted[0:1, 0:1], min_val=0, max_val=1)):
                ranked = [0]

                def rank_link(ins):
                    ranked[0] += 1
                    ins.then_inc(rank_step, 1)
                    dve.wait_ge(rank_step, ranked[0])
                find_slots("dst", rank_link)
                dve.sem_inc(dst_rank, 1)

            link(v.tensor_scalar(block_i, dst_i, 7, None, ALU.logical_shift_right))
            link(v.scalar_tensor_tensor(out=dst_low, in0=block_i, scalar=-128.0, in1=dst_i, op0=ALU.mult, op1=ALU.add))
            link(v.scalar_tensor_tensor(out=type_block, in0=type_i, scalar=float(NBLK), in1=block_i, op0=ALU.mult, op1=ALU.add))
            dve.sem_inc(keys_ready, 1)
            o = R * NBLK

            def hot_turn(i, peeled=False):
                for u in range(CU):
                    if not peeled:
                        dve.wait_ge(counted, CU * i + u + 1 - CU)
                    last = v.tensor_scalar(hot[:, u, 0:o], iota16[0:EP, 0:o], type_block[:, bass.ds(CU * i + u, 1)], None, ALU.is_equal)
                    if u % CU2 >= BY_ACT:
                        last = v.tensor_scalar(hot[:, u, o:o + 128], iota16[0:EP, 0:128], dst_low[:, bass.ds(CU * i + u, 1)], None, ALU.is_equal)
                    last.then_inc(hot_ready, 1)
            hot_turn(0, peeled=True)
            with dve.Fori(1, EC // CU) as i:
                hot_turn(i)
            dve.wait_ge(counted, EC + 1)

            link(v.memset(src_block, -1.0))
            link(v.memset(src_low, -1.0))
            link(v.tensor_scalar(bucket_i, src_i, 7, None, ALU.logical_shift_right))
            link(v.tensor_copy(src_block[:, 0:EC], bucket_i))
            link(v.scalar_tensor_tensor(out=src_low[:, 0:EC], in0=bucket_i, scalar=-128.0, in1=src_i, op0=ALU.mult, op1=ALU.add))

            link(v.tensor_scalar(inv_f, psum[:, 4, 0:R * NBLK], 1.0, None, ALU.max))
            v.reciprocal(inv_f, inv_f).then_inc(inv_found, 1)
            v.memset(inv_count, 0.0).then_inc(inv_clear, 1)
            dve.wait_ge(inv_turned, 1)
            turned = psum[0:CROW, 5, :]
            link(v.tensor_copy(inv_parts[:, 0, :], turned))
            link(v.tensor_tensor(rest_f, turned, inv_parts[:, 0, :], ALU.subtract))
            link(v.tensor_copy(inv_parts[:, 1, :], rest_f))
            v.tensor_tensor(inv_parts[:, 2, :], rest_f, inv_parts[:, 1, :], ALU.subtract).then_inc(inv_ready, 1)
            dve.wait_ge(x_kept, NXT)
            link(v.memset(cur[:, N:NP], 0.0))

            def keep_slots(k, n):
                dve.wait_ge(runs_turned, n + 1)
                if n == 0:
                    link(v.memset(slots[:, NT:NTP, 0], 0.0))
                    link(v.memset(slots[:, NT:NTP, 1], NODST))
                for h, (lo, hi) in enumerate(((0, BW), (BW, NT))):
                    link(v.tensor_copy(slots[:, lo:hi, 0], psum[:, h, 0:hi - lo]))
                    last = v.scalar_tensor_tensor(out=slots[:, lo:hi, 1].rearrange("p (g t) -> p g t", t=2),
                                                  in0=bucket[k][:, lo // 2:hi // 2].unsqueeze(2).to_broadcast([128, (hi - lo) // 2, 2]),
                                                  scalar=-float(HI), in1=psum[:, 2 + h, 0:hi - lo].rearrange("p (g t) -> p g t", t=2),
                                                  op0=ALU.mult, op1=ALU.add)
                    if h == 0:
                        link(last)
                last.then_inc(slots_ready, 1)
                dve.wait_ge(slots_ready, n + 1)

            def table(layer):
                for nb in range(NBLK):
                    n = NBLK * layer + nb
                    dve.wait_ge(table_mm, n + 1)
                    if n >= 4:
                        dve.wait_ge(table_out[n % 4], 16 * (n // 4))
                    v.tensor_copy(table_stage[:, n % 4, 512:1024], psum[:, 2 * (n % 3) + 1, :]).then_inc(table_dve, 1)

            def conv(k):
                width = D if k < LAYERS else H
                which = "dst" if k < LAYERS else "src"
                if k < LAYERS:
                    for s in range(4):
                        dve.wait_ge(table_out[s], 16 * len(range(s, NBLK * (k + 1), 4)))
                    dve.wait_ge(root_kept, NB * (k + 1))
                else:
                    for m in range(NHB):
                        dve.wait_ge(hop_out[m], 16 * (k - LAYERS + 1))

                def select(i, b):
                    dve.wait_ge(summed, B + tiles(k, i, b) + 1 - SB)
                    column = bass.ds(B * i + b, 1)
                    weight = (norm[:, column], ALU.is_equal, ALU.mult) if k < LAYERS else (None, ALU.is_equal)
                    v.tensor_scalar(sel[:, b % SB, :], iota[:, :], slots[:, column, 1], *weight).then_inc(sel_ready, 1)
                    if k < LAYERS and b < DC:
                        at = DC * (NIT * k + i) + b
                        dve.wait_ge(degrees, at + 1)
                        u = degree_hot[:, b, :]
                        v.tensor_scalar(u[:, 0:NBLK], iota16[0:EP, 0:NBLK], src_block[:, bass.ds(at, 1)], None, ALU.is_equal)
                        v.tensor_scalar(u[:, NBLK + 1:NBLK + 129], iota16[0:EP, 0:128], src_low[:, bass.ds(at, 1)], None,
                                        ALU.is_equal).then_inc(degree_ready, 1)

                def add(i, q):
                    column = dve.value_load(bucket[which][0:1, bass.ds(Q * i + q, 1)], min_val=0, max_val=(NB - 1) * 128)
                    dve.wait_ge(summed, B + tiles(k, i) + 2 * q + 2)
                    dve.wait_ge(added, PB + groups_of(k, i, q))
                    at = agg[0:width, bass.ds(column * HI, BW)]
                    v.tensor_tensor(at, at, psum[0:width, q % PB, :], ALU.add).then_inc(added, 1)

                def turn(i, n, first=False):
                    for q in range(n // 2):
                        select(i, 2 * q)
                        select(i, 2 * q + 1)
                        if q >= 2 or not first:
                            add(i, q - 2)
                turn(0, B, first=True)
                with dve.Fori(1, NIT - 1) as i:
                    turn(i, B)
                turn(NIT - 1, LAST_B)
                for q in range(LAST_B // 2 - 2, LAST_B // 2):
                    add(NIT - 1, q)
                dve.wait_ge(added, PB + groups_of(k + 1, 0))

            def edge_weights():
                def hot_types_of(i, c):
                    dve.wait_ge(types_turned, WB * i + c + 1)
                    v.tensor_tensor(type_hot[:, c * CH:(c + 1) * CH, :],
                                    type_f[:, bass.ds((WB * i + c) * CH, CH)].unsqueeze(2).to_broadcast([128, CH, 3 * TH]),
                                    iota_types[:, :].unsqueeze(1).to_broadcast([128, CH, 3 * TH]), ALU.is_equal).then_inc(hot_types, 1)

                def take(i, c):
                    dve.wait_ge(weight_rows, WB + WB * i + c + 1)
                    dve.wait_ge(norms, WB * i + c + 1)
                    for j in range(CH):
                        at = bass.ds((WB * i + c) * CH + j, 1)
                        last = v.scalar_tensor_tensor(out=unread[:, c * CH + j, :], in0=iota[:, 0:128], scalar=low_f[:, at],
                                                      in1=psum[:, c, j * 128:(j + 1) * 128], op0=ALU.is_equal, op1=ALU.mult,
                                                      accum_out=norm[:, at])
                    last.then_inc(norms, 1)
                for c in range(WB):
                    hot_types_of(0, c)
                turns, rest = divmod(NCHUNK, WB)
                with dve.Fori(1, turns) as i:
                    for c in range(WB):
                        hot_types_of(i, c)
                        take(i - 1, c)
                for c in range(WB):
                    if c < rest:
                        hot_types_of(turns, c)
                    take(turns - 1, c)
                for c in range(rest):
                    take(turns, c)
                dve.wait_ge(norms, WB + NCHUNK)

            def normalise(n, other):
                base = NB * n
                for c in range(NB):
                    if n:
                        dve.wait_ge(out_biased, c + 1)
                    v.tensor_tensor(agg[:, chunk[c]], xT[:, chunk[c]], other[:, chunk[c]], ALU.add).then_inc(ln_in, 1)

                def find_moments(c):
                    dve.wait_ge(ln_turned, base + c + 1)
                    for j in range(len(blocks_of[c])):
                        last = v.bn_stats(node_stats[:, c % 2, j, :], psum[:, c % 4, j * 128:(j + 1) * 128])
                    link(last)
                    for j, nb in enumerate(blocks_of[c]):
                        last = v.bn_aggr(node_moments[:, nb, :], node_stats[:, c % 2, j, :])
                    last.then_inc(ln_var, 1)

                def scale_rows(c):
                    dve.wait_ge(ln_std, base + c + 1)
                    bl = blocks_of[c]
                    here = deviation[:, bl[0]:bl[-1] + 1]
                    link(v.reciprocal(here, here))
                    if n == 0 and c >= 4:
                        dve.wait_ge(ln_back, c - 3)
                    for j, nb in enumerate(bl):
                        to = sel[:, c % 4, j * 128:(j + 1) * 128] if n == 0 else cur[:, nb * 128:(nb + 1) * 128]
                        last = v.tensor_scalar(to, psum[:, c % 4, j * 128:(j + 1) * 128], node_moments[:, nb, 0:1],
                                               deviation[:, nb:nb + 1], ALU.subtract, ALU.mult)
                    last.then_inc(ln_rows, 1)
                for c in range(NB + 1):
                    if c < NB:
                        find_moments(c)
                    if c:
                        scale_rows(c - 1)

            keep_slots("dst", 0)
            link(v.tensor_copy(type_t, slots[:, :, 0]))
            link(v.tensor_scalar(type_t, type_t, R - 1, None, ALU.bitwise_and))
            link(v.tensor_copy(key_t, slots[:, :, 1]))
            link(v.tensor_scalar(high_t, key_t, 7, None, ALU.logical_shift_right))
            link(v.tensor_scalar(key_t, key_t, 127, None, ALU.bitwise_and))
            link(v.scalar_tensor_tensor(out=type_f, in0=type_t, scalar=float(HI), in1=high_t, op0=ALU.mult, op1=ALU.add))
            link(v.tensor_copy(low_f, key_t))
            edge_weights()
            for layer in range(LAYERS):
                if layer + 1 < LAYERS:
                    make_weights(layer + 1)
                conv(layer)
                if layer == 0:
                    v.memset(bufE[0:H, NROW:NP], 0.0).then_inc(scale_clear, 1)
                if layer == LAYERS - 1:
                    break
                for c in range(NB):
                    last = v.bn_stats(stats[:, c, :], agg[:, live[c]])
                link(last)
                v.bn_aggr(moments[:, :], stats[:, :, :].rearrange("p c s -> p (c s)")).then_inc(var_ready, 1)
                dve.wait_ge(std_ready, layer + 1)
                link(v.reciprocal(affine[:, 1:2], affine[:, 0:1]))
                link(v.tensor_tensor(affine[:, 2:3], affine[:, 1:2], bn_sb[:, 0, layer:layer + 1], ALU.mult))
                link(v.tensor_tensor(affine[:, 0:1], moments[:, 0:1], affine[:, 2:3], ALU.mult))
                v.tensor_tensor(affine[:, 3:4], bn_sb[:, 1, layer:layer + 1], affine[:, 0:1], ALU.subtract).then_inc(affine_ready, 1)
                table(layer + 1)
            dve.wait_ge(degrees, DC + DCOLS + 1)
            link(v.tensor_copy(deg_f, psum[0:NBLK, 7, 0:128]))
            v.tensor_scalar(deg_r, deg_f, 1.0, None, ALU.max).then_inc(deg_ready, 1)
            dve.wait_ge(root_ready, 1)
            link(v.reciprocal(deg_r, deg_r))
            v.scalar_tensor_tensor(out=deg_out, in0=deg_f, scalar=0.0, in1=deg_r, op0=ALU.is_gt, op1=ALU.mult).then_inc(deg_done, 1)
            keep_slots("src", 1)
            normalise(0, agg)

            dve.wait_ge(scale_in, 16)
            scale, sums, scaled, edge_sums = bufE[0:H, :], bufD[0:H, :], cur[0:H, :], agg[0:H, :]
            for c in range(NB):
                dve.wait_ge(proj_kept, c + 1)
                v.tensor_tensor(scaled[:, chunk[c]], scaled[:, chunk[c]], scale[:, chunk[c]], ALU.mult).then_inc(hop_scaled, 1)
            dve.wait_ge(hop_scaled, NB)
            link(v.tensor_tensor(scale, scale, scale, ALU.mult))
            for hop in range(HOPS):
                link(v.memset(edge_sums, 0.0))
                conv(LAYERS + hop)
                if hop == HOPS - 1:
                    break
                for c in range(NB):
                    v.tensor_tensor(scaled[:, chunk[c]], edge_sums[:, chunk[c]], scale[:, chunk[c]], ALU.mult).then_inc(hop_scaled, 1)
                if hop == 0:
                    link(v.tensor_copy(sums, edge_sums))
                else:
                    link(v.tensor_tensor(sums, sums, edge_sums, ALU.add))
                if hop == HOPS - 2:
                    dve.wait_ge(hop_scaled, NB * HOPS)
                    dve.sem_inc(squares_used, 1)
            dve.wait_ge(scale_in, 32)
            for c in range(NB):
                link(v.tensor_tensor(sums[:, chunk[c]], sums[:, chunk[c]], edge_sums[:, chunk[c]], ALU.add))
                v.tensor_tensor(sums[:, chunk[c]], sums[:, chunk[c]], scale[:, chunk[c]], ALU.mult).then_inc(hop_scaled, 1)
            normalise(1, cur)


_INS = ["x", "src", "dst", "edge_type_8", "L0_gnn_bases", "L0_gnn_comp", "L0_gnn_root", "L0_gnn_bias", "L0_gnn_bn_weight",
        "L0_gnn_bn_bias", "L1_gnn_W_in", "L1_gnn_b_in", "L1_gnn_W_out", "L1_gnn_b_out"]


def kernel(**inputs):
    import concourse.bacc as bacc
    from concourse.bass_utils import run_bass_kernel_spmd

    nc = bacc.Bacc("TRN2", target_bir_lowering=False, num_devices=1)
    arrays, args = {}, []
    for name in _INS:
        a = np.ascontiguousarray(inputs[name])
        arrays[f"in_{name}"] = a
        args.append(nc.dram_tensor(f"in_{name}", a.shape, mybir.dt.from_np(a.dtype), kind="ExternalInput").ap())
    args.append(nc.dram_tensor("out", (N, D), F32, kind="ExternalOutput").ap())
    build(nc, *args)
    return run_bass_kernel_spmd(nc, [arrays], core_ids=[0]).results[0]["out"]
```
